# Optimizing a Trainium2 kernel written in Bass

```python
import numpy as np
import jax
import jax.numpy as jnp

def _softmax(x, axis=-1):
    return jax.nn.softmax(x, axis=axis)

def _gelu(x):
    return jax.nn.gelu(x, approximate=True)

def _silu(x):
    return jax.nn.silu(x)

def _sigmoid(x):
    return jax.nn.sigmoid(x)

def _layernorm(x, axis=-1, eps=1e-05):
    m = jnp.mean(x, axis=axis, keepdims=True)
    v = jnp.var(x, axis=axis, keepdims=True)
    return (x - m) / jnp.sqrt(v + eps)

def _scatter_add(tgt, idx, src, axis=0):
    return tgt.at[idx].add(src)

def _segment_sum(src, seg, n):
    return jax.ops.segment_sum(src, seg, n)
kernel_name = 'mk_pixart_seq_d2_seqx_r4_36a305'

def setup_inputs(seed: int=0):
    np.random.seed(seed)
    _w = jnp.asarray

    def _rec_inputs():
        import jax
        import jax.numpy as jnp
        _rk = jax.random.key(seed)
        x = -0.0005207 + 1.001 * jax.random.normal(jax.random.fold_in(_rk, 1), (8, 256, 256), jnp.float32)
        _lenS = 256 - jax.random.randint(jax.random.fold_in(_rk, 7), (8,), 0, max(1, 256 // 4) + 1, jnp.int32)
        _lenS2 = 120 - jax.random.randint(jax.random.fold_in(_rk, 8), (8,), 0, max(1, 120 // 4) + 1, jnp.int32)
        cond_1024 = 0.000887014 + 1.03683 * jax.random.normal(jax.random.fold_in(_rk, 11), (8, 256), jnp.float32)
        _ctx_768P = jax.random.normal(jax.random.fold_in(_rk, 12), (8, 16, 192), jnp.float32)
        _ctx_768c = jax.random.dirichlet(jax.random.fold_in(_rk, 512), 0.3 * jnp.ones((16,), jnp.float32), (8, 120))
        _ctx_768t = jnp.einsum('bsk,bkd->bsd', _ctx_768c, _ctx_768P)
        _ctx_768t = _ctx_768t * jax.lax.rsqrt(jnp.mean(jnp.square(_ctx_768t)) + 1e-12) * 0.953939
        ctx_768 = 0.000599585 + 1.00006 * (_ctx_768t + 0.3 * jax.random.normal(jax.random.fold_in(_rk, 612), (8, 120, 192), jnp.float32))
        return (x, cond_1024, ctx_768)
    x, cond_1024, ctx_768 = _rec_inputs()

    def _L0_xcond_setup():
        import jax, jax.numpy as jnp
        import numpy as np
        B, N, M = (2, 256, 128)
        D, H, DH = (256, 16, 64)
        MID = H * DH
        DC = 192
        MULT = 4
        EPS = 1e-05

        def _ln(x, w, b):
            mu = jnp.mean(x, -1, keepdims=True)
            var = jnp.mean((x - mu) ** 2, -1, keepdims=True)
            return (x - mu) * jax.lax.rsqrt(var + EPS) * w + b

        def _sincos(n, d):
            inv = 1.0 / 10000.0 ** (jnp.arange(0, d, 2, dtype=jnp.float32) / d)
            ang = jnp.arange(n, dtype=jnp.float32)[:, None] * inv[None, :]
            return (jnp.sin(ang), jnp.cos(ang))

        def _rope(x, sin, cos):
            s = sin[None, None]
            c = cos[None, None]
            xe = x[..., ::2]
            xo = x[..., 1::2]
            re = xe * c - xo * s
            ro = xe * s + xo * c
            return jnp.stack((re, ro), axis=-1).reshape(x.shape)

        def _heads(t):
            b, n, _ = t.shape
            return t.reshape(b, n, H, DH).transpose(0, 2, 1, 3)

        def _attn(xq, ctx, wq, wkv, wo, bo):
            q = _heads(xq @ wq)
            k, v = jnp.split(ctx @ wkv, 2, axis=-1)
            k = _heads(k)
            v = _heads(v)
            sq, cq = _sincos(q.shape[2], DH)
            sk, ck = _sincos(k.shape[2], DH)
            q = _rope(q, sq, cq)
            k = _rope(k, sk, ck)
            sim = jnp.einsum('bhnd,bhmd->bhnm', q, k) * DH ** (-0.5)
            a = jax.nn.softmax(sim, axis=-1)
            o = jnp.einsum('bhnm,bhmd->bhnd', a, v)
            o = o.transpose(0, 2, 1, 3).reshape(xq.shape[0], xq.shape[1], MID)
            return o @ wo + bo

        def _adaln(x, c, lw, lb, gw, gb, bw, bb):
            g = (c @ gw + gb)[:, None, :]
            bt = (c @ bw + bb)[:, None, :]
            return _ln(x, lw, lb) * (1.0 + g) + bt
        ks = jax.random.split(jax.random.key(seed), 24)
        s = 0.02
        inp = {'x': jax.random.normal(ks[0], (B, N, D), jnp.float32), 'cond': jax.random.normal(ks[1], (B, D), jnp.float32), 'context': jax.random.normal(ks[2], (B, M, DC), jnp.float32), 'ln1_w': jnp.ones((D,), jnp.float32), 'ln1_b': jnp.zeros((D,), jnp.float32), 'g1_w': jax.random.normal(ks[3], (D, D), jnp.float32) * s, 'g1_b': jnp.zeros((D,), jnp.float32), 'b1_w': jax.random.normal(ks[4], (D, D), jnp.float32) * s, 'b1_b': jnp.zeros((D,), jnp.float32), 'ln2_w': jnp.ones((D,), jnp.float32), 'ln2_b': jnp.zeros((D,), jnp.float32), 'g2_w': jax.random.normal(ks[5], (D, D), jnp.float32) * s, 'g2_b': jnp.zeros((D,), jnp.float32), 'b2_w': jax.random.normal(ks[6], (D, D), jnp.float32) * s, 'b2_b': jnp.zeros((D,), jnp.float32), 'sa_wq': jax.random.normal(ks[7], (D, MID), jnp.float32) * s, 'sa_wkv': jax.random.normal(ks[8], (D, 2 * MID), jnp.float32) * s, 'sa_wo': jax.random.normal(ks[9], (MID, D), jnp.float32) * s, 'sa_bo': jnp.zeros((D,), jnp.float32), 'ca_lnc_w': jnp.ones((DC,), jnp.float32), 'ca_lnc_b': jnp.zeros((DC,), jnp.float32), 'ca_wq': jax.random.normal(ks[10], (D, MID), jnp.float32) * s, 'ca_wkv': jax.random.normal(ks[11], (DC, 2 * MID), jnp.float32) * s, 'ca_wo': jax.random.normal(ks[12], (MID, D), jnp.float32) * s, 'ca_bo': jnp.zeros((D,), jnp.float32), 'ff_w1': jax.random.normal(ks[13], (D, MULT * D), jnp.float32) * s, 'ff_b1': jnp.zeros((MULT * D,), jnp.float32), 'ff_w2': jax.random.normal(ks[14], (MULT * D, D), jnp.float32) * s, 'ff_b2': jnp.zeros((D,), jnp.float32)}
        return inp
    _L0_xcond_all = _L0_xcond_setup()
    _L0_xcond_in = {k: v for k, v in _L0_xcond_all.items() if k in ('ln1_w', 'ln1_b', 'g1_w', 'g1_b', 'b1_w', 'b1_b', 'ln2_w', 'ln2_b', 'g2_w', 'g2_b', 'b2_w', 'b2_b', 'sa_wq', 'sa_wkv', 'sa_wo', 'sa_bo', 'ca_lnc_w', 'ca_lnc_b', 'ca_wq', 'ca_wkv', 'ca_wo', 'ca_bo', 'ff_w1', 'ff_b1', 'ff_w2', 'ff_b2')}
    del _L0_xcond_all

    def _L1_xcond_setup():
        import jax, jax.numpy as jnp
        import numpy as np
        B, N, D, H, TD, TL = (4, 256, 256, 16, 192, 77)
        HD = D // H
        EPS = 1e-06

        def _ln(x):
            mu = jnp.mean(x, axis=-1, keepdims=True)
            var = jnp.var(x, axis=-1, keepdims=True)
            return (x - mu) * jax.lax.rsqrt(var + EPS)

        def _modulate(x, shift, scale):
            return x * (1.0 + scale[:, None, :]) + shift[:, None, :]

        def _heads(t):
            return t.reshape(t.shape[0], t.shape[1], H, HD).transpose(0, 2, 1, 3)

        def _attend(q, k, v):
            sim = jnp.einsum('bhid,bhjd->bhij', q, k) * HD ** (-0.5)
            attn = jax.nn.softmax(sim, axis=-1)
            out = jnp.einsum('bhij,bhjd->bhid', attn, v)
            return out.transpose(0, 2, 1, 3).reshape(out.shape[0], -1, D)
        key = jax.random.key(seed)
        ks = jax.random.split(key, 16)
        s = 0.02
        return {'x': jax.random.normal(ks[0], (B, N, D), jnp.float32), 'c': jax.random.normal(ks[1], (B, D), jnp.float32), 'text_embed': jax.random.normal(ks[2], (B, TL, TD), jnp.float32), 'W_ada': jax.random.normal(ks[3], (D, 6 * D), jnp.float32) * s, 'b_ada': jnp.zeros((6 * D,), jnp.float32), 'W_qkv': jax.random.normal(ks[4], (D, 3 * D), jnp.float32) * s, 'b_qkv': jnp.zeros((3 * D,), jnp.float32), 'W_proj': jax.random.normal(ks[5], (D, D), jnp.float32) * s, 'b_proj': jnp.zeros((D,), jnp.float32), 'W_ctx': jax.random.normal(ks[6], (TD, D), jnp.float32) * s, 'b_ctx': jnp.zeros((D,), jnp.float32), 'W_q': jax.random.normal(ks[7], (D, D), jnp.float32) * s, 'W_k': jax.random.normal(ks[8], (D, D), jnp.float32) * s, 'W_v': jax.random.normal(ks[9], (D, D), jnp.float32) * s, 'W_out': jax.random.normal(ks[10], (D, D), jnp.float32) * s, 'b_out': jnp.zeros((D,), jnp.float32), 'W_fc1': jax.random.normal(ks[11], (D, 4 * D), jnp.float32) * s, 'b_fc1': jnp.zeros((4 * D,), jnp.float32), 'W_fc2': jax.random.normal(ks[12], (4 * D, D), jnp.float32) * s, 'b_fc2': jnp.zeros((D,), jnp.float32)}
    _L1_xcond_all = _L1_xcond_setup()
    _L1_xcond_in = {k: v for k, v in _L1_xcond_all.items() if k in ('W_ada', 'b_ada', 'W_qkv', 'b_qkv', 'W_proj', 'b_proj', 'W_ctx', 'b_ctx', 'W_q', 'W_k', 'W_v', 'W_out', 'b_out', 'W_fc1', 'b_fc1', 'W_fc2', 'b_fc2')}
    del _L1_xcond_all
    return {'x': x, 'cond_1024': cond_1024, 'ctx_768': ctx_768, 'L0_xcond_ln1_w': _L0_xcond_in['ln1_w'], 'L0_xcond_ln1_b': _L0_xcond_in['ln1_b'], 'L0_xcond_g1_w': _L0_xcond_in['g1_w'], 'L0_xcond_g1_b': _L0_xcond_in['g1_b'], 'L0_xcond_b1_w': _L0_xcond_in['b1_w'], 'L0_xcond_b1_b': _L0_xcond_in['b1_b'], 'L0_xcond_ln2_w': _L0_xcond_in['ln2_w'], 'L0_xcond_ln2_b': _L0_xcond_in['ln2_b'], 'L0_xcond_g2_w': _L0_xcond_in['g2_w'], 'L0_xcond_g2_b': _L0_xcond_in['g2_b'], 'L0_xcond_b2_w': _L0_xcond_in['b2_w'], 'L0_xcond_b2_b': _L0_xcond_in['b2_b'], 'L0_xcond_sa_wq': _L0_xcond_in['sa_wq'], 'L0_xcond_sa_wkv': _L0_xcond_in['sa_wkv'], 'L0_xcond_sa_wo': _L0_xcond_in['sa_wo'], 'L0_xcond_sa_bo': _L0_xcond_in['sa_bo'], 'L0_xcond_ca_lnc_w': _L0_xcond_in['ca_lnc_w'], 'L0_xcond_ca_lnc_b': _L0_xcond_in['ca_lnc_b'], 'L0_xcond_ca_wq': _L0_xcond_in['ca_wq'], 'L0_xcond_ca_wkv': _L0_xcond_in['ca_wkv'], 'L0_xcond_ca_wo': _L0_xcond_in['ca_wo'], 'L0_xcond_ca_bo': _L0_xcond_in['ca_bo'], 'L0_xcond_ff_w1': _L0_xcond_in['ff_w1'], 'L0_xcond_ff_b1': _L0_xcond_in['ff_b1'], 'L0_xcond_ff_w2': _L0_xcond_in['ff_w2'], 'L0_xcond_ff_b2': _L0_xcond_in['ff_b2'], 'L1_xcond_W_ada': _L1_xcond_in['W_ada'], 'L1_xcond_b_ada': _L1_xcond_in['b_ada'], 'L1_xcond_W_qkv': _L1_xcond_in['W_qkv'], 'L1_xcond_b_qkv': _L1_xcond_in['b_qkv'], 'L1_xcond_W_proj': _L1_xcond_in['W_proj'], 'L1_xcond_b_proj': _L1_xcond_in['b_proj'], 'L1_xcond_W_ctx': _L1_xcond_in['W_ctx'], 'L1_xcond_b_ctx': _L1_xcond_in['b_ctx'], 'L1_xcond_W_q': _L1_xcond_in['W_q'], 'L1_xcond_W_k': _L1_xcond_in['W_k'], 'L1_xcond_W_v': _L1_xcond_in['W_v'], 'L1_xcond_W_out': _L1_xcond_in['W_out'], 'L1_xcond_b_out': _L1_xcond_in['b_out'], 'L1_xcond_W_fc1': _L1_xcond_in['W_fc1'], 'L1_xcond_b_fc1': _L1_xcond_in['b_fc1'], 'L1_xcond_W_fc2': _L1_xcond_in['W_fc2'], 'L1_xcond_b_fc2': _L1_xcond_in['b_fc2']}

def reference(x, cond_1024, ctx_768, L0_xcond_ln1_w, L0_xcond_ln1_b, L0_xcond_g1_w, L0_xcond_g1_b, L0_xcond_b1_w, L0_xcond_b1_b, L0_xcond_ln2_w, L0_xcond_ln2_b, L0_xcond_g2_w, L0_xcond_g2_b, L0_xcond_b2_w, L0_xcond_b2_b, L0_xcond_sa_wq, L0_xcond_sa_wkv, L0_xcond_sa_wo, L0_xcond_sa_bo, L0_xcond_ca_lnc_w, L0_xcond_ca_lnc_b, L0_xcond_ca_wq, L0_xcond_ca_wkv, L0_xcond_ca_wo, L0_xcond_ca_bo, L0_xcond_ff_w1, L0_xcond_ff_b1, L0_xcond_ff_w2, L0_xcond_ff_b2, L1_xcond_W_ada, L1_xcond_b_ada, L1_xcond_W_qkv, L1_xcond_b_qkv, L1_xcond_W_proj, L1_xcond_b_proj, L1_xcond_W_ctx, L1_xcond_b_ctx, L1_xcond_W_q, L1_xcond_W_k, L1_xcond_W_v, L1_xcond_W_out, L1_xcond_b_out, L1_xcond_W_fc1, L1_xcond_b_fc1, L1_xcond_W_fc2, L1_xcond_b_fc2):
    import jax
    import jax.numpy as jnp

    def _L0_xcond_ref(x, cond, context, ln1_w, ln1_b, g1_w, g1_b, b1_w, b1_b, ln2_w, ln2_b, g2_w, g2_b, b2_w, b2_b, sa_wq, sa_wkv, sa_wo, sa_bo, ca_lnc_w, ca_lnc_b, ca_wq, ca_wkv, ca_wo, ca_bo, ff_w1, ff_b1, ff_w2, ff_b2):
        import jax, jax.numpy as jnp
        import numpy as np
        B, N, M = (2, 256, 128)
        D, H, DH = (256, 16, 64)
        MID = H * DH
        DC = 192
        MULT = 4
        EPS = 1e-05

        def _ln(x, w, b):
            mu = jnp.mean(x, -1, keepdims=True)
            var = jnp.mean((x - mu) ** 2, -1, keepdims=True)
            return (x - mu) * jax.lax.rsqrt(var + EPS) * w + b

        def _sincos(n, d):
            inv = 1.0 / 10000.0 ** (jnp.arange(0, d, 2, dtype=jnp.float32) / d)
            ang = jnp.arange(n, dtype=jnp.float32)[:, None] * inv[None, :]
            return (jnp.sin(ang), jnp.cos(ang))

        def _rope(x, sin, cos):
            s = sin[None, None]
            c = cos[None, None]
            xe = x[..., ::2]
            xo = x[..., 1::2]
            re = xe * c - xo * s
            ro = xe * s + xo * c
            return jnp.stack((re, ro), axis=-1).reshape(x.shape)

        def _heads(t):
            b, n, _ = t.shape
            return t.reshape(b, n, H, DH).transpose(0, 2, 1, 3)

        def _attn(xq, ctx, wq, wkv, wo, bo):
            q = _heads(xq @ wq)
            k, v = jnp.split(ctx @ wkv, 2, axis=-1)
            k = _heads(k)
            v = _heads(v)
            sq, cq = _sincos(q.shape[2], DH)
            sk, ck = _sincos(k.shape[2], DH)
            q = _rope(q, sq, cq)
            k = _rope(k, sk, ck)
            sim = jnp.einsum('bhnd,bhmd->bhnm', q, k) * DH ** (-0.5)
            a = jax.nn.softmax(sim, axis=-1)
            o = jnp.einsum('bhnm,bhmd->bhnd', a, v)
            o = o.transpose(0, 2, 1, 3).reshape(xq.shape[0], xq.shape[1], MID)
            return o @ wo + bo

        def _adaln(x, c, lw, lb, gw, gb, bw, bb):
            g = (c @ gw + gb)[:, None, :]
            bt = (c @ bw + bb)[:, None, :]
            return _ln(x, lw, lb) * (1.0 + g) + bt
        attn_in = _adaln(x, cond, ln1_w, ln1_b, g1_w, g1_b, b1_w, b1_b)
        x = _attn(attn_in, attn_in, sa_wq, sa_wkv, sa_wo, sa_bo) + x
        cross_in = _adaln(x, cond, ln1_w, ln1_b, g1_w, g1_b, b1_w, b1_b)
        ctx_n = _ln(context, ca_lnc_w, ca_lnc_b)
        x = _attn(cross_in, ctx_n, ca_wq, ca_wkv, ca_wo, ca_bo) + x
        ffn_in = _adaln(x, cond, ln2_w, ln2_b, g2_w, g2_b, b2_w, b2_b)
        h = jax.nn.gelu(ffn_in @ ff_w1 + ff_b1, approximate=False)
        x = h @ ff_w2 + ff_b2 + x
        return x

    def _L1_xcond_ref(x, c, text_embed, W_ada, b_ada, W_qkv, b_qkv, W_proj, b_proj, W_ctx, b_ctx, W_q, W_k, W_v, W_out, b_out, W_fc1, b_fc1, W_fc2, b_fc2):
        import jax, jax.numpy as jnp
        import numpy as np
        B, N, D, H, TD, TL = (4, 256, 256, 16, 192, 77)
        HD = D // H
        EPS = 1e-06

        def _ln(x):
            mu = jnp.mean(x, axis=-1, keepdims=True)
            var = jnp.var(x, axis=-1, keepdims=True)
            return (x - mu) * jax.lax.rsqrt(var + EPS)

        def _modulate(x, shift, scale):
            return x * (1.0 + scale[:, None, :]) + shift[:, None, :]

        def _heads(t):
            return t.reshape(t.shape[0], t.shape[1], H, HD).transpose(0, 2, 1, 3)

        def _attend(q, k, v):
            sim = jnp.einsum('bhid,bhjd->bhij', q, k) * HD ** (-0.5)
            attn = jax.nn.softmax(sim, axis=-1)
            out = jnp.einsum('bhij,bhjd->bhid', attn, v)
            return out.transpose(0, 2, 1, 3).reshape(out.shape[0], -1, D)
        mod = jax.nn.silu(c) @ W_ada + b_ada
        sh_msa, sc_msa, sh_x, sc_x, sh_mlp, sc_mlp = jnp.split(mod, 6, axis=-1)
        h1 = _modulate(_ln(x), sh_msa, sc_msa)
        qkv = h1 @ W_qkv + b_qkv
        q, k, v = jnp.split(qkv, 3, axis=-1)
        out = _attend(_heads(q), _heads(k), _heads(v))
        x = x + (out @ W_proj + b_proj)
        h2 = _modulate(_ln(x), sh_x, sc_x)
        ctx = text_embed @ W_ctx + b_ctx
        q = _heads(h2 @ W_q)
        k = _heads(ctx @ W_k)
        v = _heads(ctx @ W_v)
        out = _attend(q, k, v)
        x = x + (out @ W_out + b_out)
        h3 = _modulate(_ln(x), sh_mlp, sc_mlp)
        hidden = jax.nn.gelu(h3 @ W_fc1 + b_fc1, approximate=True)
        x = x + (hidden @ W_fc2 + b_fc2)
        return x
    x = _L0_xcond_ref(x, cond_1024, ctx_768, L0_xcond_ln1_w, L0_xcond_ln1_b, L0_xcond_g1_w, L0_xcond_g1_b, L0_xcond_b1_w, L0_xcond_b1_b, L0_xcond_ln2_w, L0_xcond_ln2_b, L0_xcond_g2_w, L0_xcond_g2_b, L0_xcond_b2_w, L0_xcond_b2_b, L0_xcond_sa_wq, L0_xcond_sa_wkv, L0_xcond_sa_wo, L0_xcond_sa_bo, L0_xcond_ca_lnc_w, L0_xcond_ca_lnc_b, L0_xcond_ca_wq, L0_xcond_ca_wkv, L0_xcond_ca_wo, L0_xcond_ca_bo, L0_xcond_ff_w1, L0_xcond_ff_b1, L0_xcond_ff_w2, L0_xcond_ff_b2)
    x = _L1_xcond_ref(x, cond_1024, ctx_768, L1_xcond_W_ada, L1_xcond_b_ada, L1_xcond_W_qkv, L1_xcond_b_qkv, L1_xcond_W_proj, L1_xcond_b_proj, L1_xcond_W_ctx, L1_xcond_b_ctx, L1_xcond_W_q, L1_xcond_W_k, L1_xcond_W_v, L1_xcond_W_out, L1_xcond_b_out, L1_xcond_W_fc1, L1_xcond_b_fc1, L1_xcond_W_fc2, L1_xcond_b_fc2)
    return x

_drawn_inputs = setup_inputs


def setup_inputs(seed=0):
    import zlib

    import numpy as np

    out = dict(_drawn_inputs(seed))
    spreads = {'L0_xcond_ln1_w': (1.0, 0.6),
     'L0_xcond_ln1_b': (0.0, 0.385),
     'L0_xcond_g1_b': (0.0, 0.8),
     'L0_xcond_b1_b': (0.0, 0.362),
     'L0_xcond_ln2_w': (1.0, 0.6),
     'L0_xcond_ln2_b': (0.0, 0.65),
     'L0_xcond_g2_b': (0.0, 0.705),
     'L0_xcond_b2_b': (0.0, 0.775),
     'L0_xcond_sa_bo': (0.0, 0.1),
     'L0_xcond_ca_lnc_w': (1.0, 0.6),
     'L0_xcond_ca_lnc_b': (0.0, 0.538),
     'L0_xcond_ca_bo': (0.0, 0.1),
     'L0_xcond_ff_b1': (0.0, 0.1),
     'L0_xcond_ff_b2': (0.0, 0.1),
     'L1_xcond_b_ada': (0.0, 0.44),
     'L1_xcond_b_qkv': (0.0, 0.278),
     'L1_xcond_b_proj': (0.0, 0.1),
     'L1_xcond_b_ctx': (0.0, 0.8),
     'L1_xcond_b_out': (0.0, 0.1),
     'L1_xcond_b_fc1': (0.0, 0.477),
     'L1_xcond_b_fc2': (0.0, 0.1)}
    factors = {'L0_xcond_g1_w': 7.423,
     'L0_xcond_sa_wq': 8.0,
     'L0_xcond_ca_wq': 8.0,
     'L1_xcond_W_ctx': 4.11,
     'L1_xcond_W_q': 8.0,
     'L1_xcond_W_k': 8.0,
     'L1_xcond_W_v': 3.161,
     'L1_xcond_W_out': 3.307}
    for name, (base, spread) in spreads.items():
        noise = np.random.default_rng([zlib.crc32(name.encode()), seed]).standard_normal(out[name].shape)
        drawn = base * np.exp(spread * noise) if base else spread * noise
        out[name] = jnp.asarray(drawn.astype(out[name].dtype))
    for name, factor in factors.items():
        out[name] = (out[name] * factor).astype(out[name].dtype)
    return out
```

```python
from contextlib import ExitStack

import numpy as np

import concourse.bass as bass
from concourse import mybir

F32 = mybir.dt.float32
ALU = mybir.AluOpType
ACT = mybir.ActivationFunctionType
AX_X = mybir.AxisListType.X

P = 128
NB, N, D = 8, 256, 256
KD = D // P
TT = N // P
H = 16
NC, DC = 120, 192
TURNS = NB // 2

COLS = {}


def _columns():
    at = 0
    for name, c in (("ln1_w", 2), ("ln1_b", 2), ("ln2_w", 2), ("ln2_b", 2), ("g1_b", 2), ("b1_b", 2),
                    ("g2_b", 2), ("b2_b", 2), ("lnc_w", 2), ("lnc_b", 2), ("ff_b1", 8), ("b_ada", 12),
                    ("b_qk", 4), ("b_ctx", 2), ("b_fc1", 8)):
        COLS[name] = at
        at += c
    return at


NCOLS = _columns()


class Stage:

    def __init__(self, nc, ctx, index, name, kind, coef, eps, DH=0, cross=False, rope=False, gelu=None,
                 shares=None):
        self.index, self.name, self.kind, self.coef, self.eps = index, name, kind, coef, eps
        self.cross, self.rope, self.gelu = cross, rope, gelu
        self.att = kind == "att"

        self.turn0 = TURNS if shares else 0
        self.b0 = NB if shares else 0
        self.loads = 48 if cross else 32

        def sem(what):
            return shares.sems[what] if shares else self.sems.setdefault(
                what, ctx.enter_context(nc.semaphore(f"{name}_{what}")))

        self.sems = {}

        self.weights_in = sem("weights_in")
        self.x_in = [sem(f"x_in{k}") for k in (0, 1)]
        self.stored = [sem(f"stored{k}") for k in (0, 1)]
        self.ln_sums = sem("ln_sums")
        self.ln_rstd = sem("ln_rstd")
        self.pool_step = sem("pool_step")
        self.dve_step = sem("dve_step")
        if rope:
            self.rope_step = sem("rope_step")
        self.xhat_ready = sem("xhat_ready")
        self.xb_ready = sem("xb_ready")
        self.h_ready = sem("h_ready")
        self.y_ready = sem("y_ready")
        self.pj_ready = sem("pj_ready")
        self.pj_free = [sem(f"pj_free{k}") for k in (0, 1)]
        if self.att:
            self.DH = DH
            self.NK = NC if cross else N
            self.KP = NC if cross else P
            self.KT = self.NK // self.KP
            self.TH = P // DH
            self.M = H * DH // P
            self.HU = 4 if cross else 2
            self.HG = 256 // DH
            self.NG = H // self.HG
            self.UI = self.HG // self.HU
            self.U = self.NG * TT * self.UI
            self.NO = self.NG * TT
            self.NQK = self.M
            self.NV = (2 * self.KT) if DH == 64 else 1
            self.s_ready = sem("s_ready")
            self.max_ready = sem("max_ready")
            self.p_ready = sem("p_ready")
            self.pt_ready = sem("pt_ready")
            self.pt_copied = sem("pt_copied")
            self.av_done = sem("av_done")
            self.o_ready = sem("o_ready")
            self.oT_done = sem("oT_done")
            self.v_ready = sem("v_ready")
            self.qk_raw = sem("qk_raw")
            self.qk_out = sem("qk_out")
            if cross:
                if rope:
                    self.ctx_sums = sem("ctx_sums")
                    self.ctx_rstd = sem("ctx_rstd")
                self.chat_ready = sem("chat_ready")
                self.cT_ready = sem("cT_ready")
                if not rope:
                    self.c_raw = sem("c_raw")
        else:
            self.g_ready = sem("g_ready")

    def first_steps(self):
        steps = [("LN", 0), ("CN", 0)] if self.cross else [("LN", 0)]
        steps += self.input_steps()
        return steps + ([("QK", j) for j in range(self.NQK)] if self.att else [])

    def input_steps(self):
        steps = [("LNT", 0)]
        if self.cross:
            steps.append(("CT", 0))
            if not self.rope:
                steps.append(("CP", 0))
        return steps

    def steps(self, last):
        if not self.att:
            out = [("LN", 1)] * (not last) + [("F1", j) for j in range(4)]
            return out + (self.input_steps() if not last else []) + [("WO", 0)]
        out = [("V", j) for j in range(self.NV)]
        due = []
        for n in range(self.U + 3):
            if n < self.U:
                out.append(("S", n))
            if 0 <= n - 2 < self.U:
                out.append(("T", n - 2))
            if 0 <= n - 3 < self.U:
                out.append(("AV", n - 3))
                if (n - 3) % self.UI == self.UI - 1:
                    due.append((n + 2, (n - 3) // self.UI))
            while due and due[0][0] <= n:
                out.append(("OT", due.pop(0)[1]))
            if n == 0 and not last:
                out += [("LN", 1)] + [("CN", 1)] * self.cross
            if n == self.U // 2 and not last:
                out += self.input_steps()
        if not last:
            out += [("QK", j) for j in range(self.NQK)]
        return out + [("OT", n) for _, n in due] + [("WO", 0)]


JOBS = ("LNT", "CT", "CP", "QK", "V", "OT", "F1", "WO")


def count_jobs(steps):
    return sum(s[0] in JOBS for s in steps)


def build(nc, x_in, ctx_in, condT, cols, ropes, rows, weights, out):
    with ExitStack() as ctx:
        def sb(name, shape):
            return ctx.enter_context(nc.sbuf_tensor(name, shape, F32))

        def sem(name):
            return ctx.enter_context(nc.semaphore(name))

        stages = [
            Stage(nc, ctx, 0, "sa0", "att", 0, 1e-5, DH=64, rope=True),
            Stage(nc, ctx, 1, "ca0", "att", 0, 1e-5, DH=64, cross=True, rope=True),
            Stage(nc, ctx, 2, "ff0", "ffn", 1, 1e-5, gelu=ACT.Gelu),
            Stage(nc, ctx, 3, "sa1", "att", 2, 1e-6, DH=16),
            Stage(nc, ctx, 4, "ca1", "att", 3, 1e-6, DH=16, cross=True),
        ]
        stages.append(Stage(nc, ctx, 5, "ff1", "ffn", 4, 1e-6, gelu=ACT.Gelu_apprx_tanh, shares=stages[2]))

        xs = [x_in] + [nc.dram_tensor(f"x_after_{st.name}", [NB, N, D], F32, kind="Internal").ap()
                       for st in stages[:-1]] + [out]
        coef_dram = nc.dram_tensor("coefs", [5, NB, P, 4], F32, kind="Internal").ap()

        WSIZE = 8192
        wbuf = [sb(f"wbuf{k}", [P, WSIZE]) for k in (0, 1)]
        colsb = sb("colsb", [P, NCOLS])
        condsb = sb("condsb", [P, KD, NB])
        silub = sb("silub", [P, KD, NB])
        esb = sb("esb", [P, KD, NB])
        modsb = sb("modsb", [P, 20, NB])
        coefsb = sb("coefsb", [P, 5, NB, 4])
        ropesb = sb("ropesb", [P, 4, N])
        rowsb = sb("rowsb", [P, 7, D])
        ident = sb("ident", [P, P])
        headmask = sb("headmask", [P, 8])
        halfpow = sb("halfpow", [P, 2])
        epsb = sb("epsb", [P, 2, TT])
        tick = sb("tick", [P, 1])
        bq4 = sb("bq4", [P, 2])

        xt = [sb(f"xt{k}", [P, TT, D]) for k in (0, 1)]
        xb = [sb(f"xb{k}", [P, TT, D]) for k in (0, 1)]
        yt = [sb(f"yt{k}", [P, TT, D]) for k in (0, 1)]
        coef = [sb(f"coef{k}", [P, 4]) for k in (0, 1)]
        ctxt = [sb(f"ctxt{k}", [P, DC]) for k in (0, 1)]
        chat = sb("chat", [P, DC])
        cT = sb("cT", [P, 2, NC])
        cRaw = sb("cRaw", [P, 2, NC])
        stats = sb("stats", [P, TT, 6])
        mv = sb("mv", [P, TT, 2])
        veps = sb("veps", [P, TT])
        rstd = sb("rstd", [P, TT])
        cstats = sb("cstats", [P, 6])
        cmv = sb("cmv", [P, 2])
        cveps = sb("cveps", [P, 1])
        crstd = sb("crstd", [P, 1])
        xhat = sb("xhat", [P, TT, D])
        hT = sb("hT", [P, KD, N])
        qT = sb("qT", [P, 8, N])
        kbd = sb("kbd", [P, H, N])
        ksb = sb("ksb", [P, 2, N])
        vaug = sb("vaug", [P, 2 * H * 65])
        sh = [sb(f"sh{k}", [P, 2 * N]) for k in (0, 1)]
        t1 = [sb(f"t1_{k}", [P, 2 * N]) for k in (0, 1)]
        negmax = [sb(f"negmax{k}", [P, 4]) for k in (0, 1)]
        prob = [sb(f"prob{k}", [P, 512]) for k in (0, 1)]
        probT = [sb(f"probT{k}", [P, 512]) for k in (0, 1)]
        rinv = [sb(f"rinv{k}", [P, H]) for k in (0, 1)]
        osb = [sb(f"osb{k}", [P, 256]) for k in (0, 1)]
        oT = sb("oT", [P, 8, N])

        def bank(name):
            return ctx.enter_context(nc.psum_tensor(name, [P, 512], F32))

        ps_s = [bank("ps_s0"), bank("ps_s1")]
        ps_t = [bank("ps_t0"), bank("ps_t1")]
        ps_o = [bank("ps_o0"), bank("ps_o1")]
        ps_j = [bank("ps_j0"), bank("ps_j1")]

        param_in = sem("param_in")
        ident_step = sem("ident_step")
        silu_step = sem("silu_step")
        mod_mm = sem("mod_mm")
        mod_step = sem("mod_step")
        coef_out = sem("coef_out")
        coef_ready = sem("coef_ready")
        mod_w_in = sem("mod_w_in")
        v_ones = sem("v_ones")
        mod_w = wbuf[1]

        def wview(st, name):
            k, n, at = weights[st.index][name][1:4]
            return wbuf[st.index % 2][:, at:at + k * n].rearrange("p (k n) -> p k n", k=k)

        def vview(st):
            return vaug[:, 0:st.KT * H * (st.DH + 1)].rearrange("p (t h d) -> p t h d", t=st.KT, h=H)

        def kview(st):
            return kbd[:, :, :].rearrange("p h n -> p (h n)")[:, 0:H * st.NK].rearrange("p (h n) -> p h n", h=H)

        class Turn:

            def __init__(self, st, i, par, job):
                self.st, self.par, self.i, self.real = st, par, i, True
                self.B = 2 * i + par
                self.per = count_jobs(st.steps(False))
                self.job = job

            def slot(self):
                j = self.job
                self.job += 1
                return j % 2, self.i * self.per + j // 2, self.i * (2 * self.per) + j + 1

        def walk(eng, st, run):
            t = Turn(st, st.turn0, 0, 0)
            t.real, t.B, t.par = False, st.b0 - 1, 1
            run(t, st.first_steps())
            base = t.job
            per = count_jobs(st.steps(False))
            with eng.Fori(0, TURNS - 1) as i:
                for par in (0, 1):
                    run(Turn(st, i + st.turn0, par, base + par * per), st.steps(False))
            for par in (0, 1):
                run(Turn(st, st.turn0 + TURNS - 1, par, base + par * per), st.steps(par == 1))

        block = ctx.enter_context(nc.Block())

        @block.sync
        def _(sp):
            sp.dma_start(colsb[:, :], cols).then_inc(param_in, 16)
            sp.dma_start(condsb[:, :, :], condT).then_inc(param_in, 16)
            sp.dma_start(ropesb[:, :, :], ropes).then_inc(param_in, 16)
            sp.dma_start(rowsb[:, :, :], rows.partition_broadcast(P)).then_inc(param_in, 16)
            for name, k, n, at, src in weights["mod"]:
                sp.dma_start(mod_w[:, at:at + k * n].rearrange("p (k n) -> p k n", k=k),
                             src.rearrange("(k p) n -> p k n", p=P)).then_inc(mod_w_in, 16)

            def load_weights(st):
                w = wbuf[st.index % 2]
                for name, (src, k, n, at) in weights[st.index].items():
                    rows_ = src.shape[0]
                    full = rows_ // P
                    sp.dma_start(w[:, at:at + full * n].rearrange("p (k n) -> p k n", k=full),
                                 src[0:full * P, :].rearrange("(k p) n -> p k n", p=P)).then_inc(st.weights_in, 16)
                    if rows_ % P:
                        sp.dma_start(w[0:rows_ % P, at + full * n:at + (full + 1) * n],
                                     src[full * P:rows_, :]).then_inc(st.weights_in, 16)

            def load_x(st, b, par, turn):
                if turn is not None:
                    sp.wait_ge(st.xhat_ready, st.b0 + b - 1)
                    sp.wait_ge(st.xb_ready, st.b0 + b - 1)
                    sp.wait_ge(st.h_ready, st.b0 + b - 1)
                sp.dma_start(xt[par][:, :, :], xs[st.index][b].rearrange("(t p) d -> p t d", p=P))\
                    .then_inc(st.x_in[par], 16)
                sp.dma_start(coef[par][:, :], coef_dram[st.coef, b]).then_inc(st.x_in[par], 16)
                if st.cross:
                    if turn is not None:
                        sp.wait_ge(st.chat_ready, b - 1)
                    sp.dma_start(ctxt[par][0:NC, :], ctx_in[b]).then_inc(st.x_in[par], 16)

            def store_y(st, b, par, i):
                sp.wait_ge(st.y_ready, st.b0 + b + 1)
                sp.dma_start(xs[st.index + 1][b].rearrange("(t p) d -> p t d", p=P), yt[par][:, :, :])\
                    .then_inc(st.stored[par], 16)

            for st in stages[0:5]:
                for par in (0, 1):
                    sp.sem_inc(st.stored[par], 1)
            load_weights(stages[0])
            sp.wait_ge(coef_ready, 1)
            sp.dma_start(coef_dram.rearrange("s b p c -> p s b c"), coefsb[:, :, :, :]).then_inc(coef_out, 16)
            sp.wait_ge(coef_out, 16)
            for st in stages:
                if st.index:
                    for par in (0, 1):
                        sp.wait_ge(stages[st.index - 1].stored[par], 16 * TURNS + 1)
                if st.index < 5:
                    load_weights(stages[st.index + 1])
                load_x(st, 0, 0, None)
                load_x(st, 1, 1, None)
                with sp.Fori(0, TURNS - 1) as i:
                    for par in (0, 1):
                        load_x(st, 2 * i + 2 + par, par, i)
                        store_y(st, 2 * i + par, par, i)
                for par in (0, 1):
                    store_y(st, NB - 2 + par, par, TURNS - 1)
            for par in (0, 1):
                sp.wait_ge(stages[-1].stored[par], 16 * (stages[-1].turn0 + TURNS) + 1)

        @block.gpsimd
        def _(pool):
            g = nc.gpsimd
            g.memset(ident[:, :], 0.0).then_inc(ident_step, 1)
            g.memset(headmask[:, :], 1.0).then_inc(ident_step, 1)
            g.memset(epsb[:, 0, :], stages[0].eps)
            g.memset(epsb[:, 1, :], stages[3].eps)
            g.memset(halfpow[:, :], -0.5).then_inc(ident_step, 1)
            g.memset(kbd[:, :, :], 0.0).then_inc(ident_step, 1)
            g.memset(vaug[:, :], 1.0).then_inc(v_ones, 1)
            pool.wait_ge(ident_step, 4)
            g.affine_select(out=ident[:, :], in_=ident[:, :], compare_op=ALU.not_equal, fill=1.0, base=0,
                            pattern=[[-1, P]], channel_multiplier=1).then_inc(ident_step, 1)
            g.affine_select(out=headmask[:, :], in_=headmask[:, :], compare_op=ALU.is_ge, fill=0.0, base=0,
                            pattern=[[-16, 8]], channel_multiplier=1).then_inc(ident_step, 1)
            pool.wait_ge(ident_step, 6)
            g.affine_select(out=headmask[:, :], in_=headmask[:, :], compare_op=ALU.is_ge, fill=0.0, base=15,
                            pattern=[[16, 8]], channel_multiplier=-1).then_inc(ident_step, 1)
            pool.wait_ge(ident_step, 7)
            pool.wait_ge(param_in, 64)

            def norm_rstd(st, t, c):
                B = t.B + 1
                par = 1 - t.par
                steps = 1 + st.cross * st.rope
                pool.wait_ge(st.ln_sums, B + 1)
                g.tensor_tensor(veps[:, :], mv[:, :, 1], epsb[:, st.index // 3, :], ALU.add).then_inc(st.pool_step, 1)
                pool.wait_ge(st.pool_step, B * steps + 1)
                g.tensor_tensor(rstd[:, :], veps[:, :], halfpow[:, :], ALU.pow).then_inc(st.ln_rstd, 1)
                turn = t.i + t.par if t.real else t.i
                pool.wait_ge(st.x_in[par], st.loads * (turn + 1))
                g.tensor_tensor(xb[par][:, :, :], xt[par][:, :, :],
                                rowsb[:, st.index, :].unsqueeze(1).to_broadcast([P, TT, D]), ALU.add)\
                    .then_inc(st.xb_ready, 1)

            def ctx_rstd_(st, t):
                B = t.B + 1
                pool.wait_ge(st.ctx_sums, B + 1)
                g.tensor_tensor(cveps[0:NC, :], cmv[0:NC, 1:2], epsb[0:NC, 0, 0:1], ALU.add).then_inc(st.pool_step, 1)
                pool.wait_ge(st.pool_step, B * 2 + 2)
                g.tensor_tensor(crstd[0:NC, :], cveps[0:NC, :], halfpow[0:NC, 0:1], ALU.pow)\
                    .then_inc(st.ctx_rstd, 1)

            def finish_qk(st, t, j):
                B = t.B + 1
                kv = kview(st)
                if st.rope:
                    half = st.NQK // 2
                    isk = j >= half
                    cols_ = st.NK if isk else N
                    m = 2 * (j % half)
                    view = lambda buf: buf[:, 0:2 * cols_].rearrange("p (m n) -> p m n", m=2)
                    pool.wait_ge(st.qk_raw, B * st.NQK + j + 1)
                    sin = ropesb[:, 3 if isk else 1, 0:cols_].unsqueeze(1).to_broadcast([P, 2, cols_])
                    g.tensor_tensor(view(sh[j % 2]), view(sh[j % 2]), sin, ALU.mult).then_inc(st.rope_step, 1)
                    pool.wait_ge(st.rope_step, B * st.NQK + j + 1)
                    if not isk:
                        g.tensor_tensor(qT[:, m:m + 2, :], view(t1[j % 2]), view(sh[j % 2]), ALU.add)\
                            .then_inc(st.qk_out, 1)
                    else:
                        for hh in (0, 1):
                            r = slice(64 * hh, 64 * hh + 64)
                            dst = kv[r, 2 * m + hh:2 * m + 4:2, :]
                            last = g.tensor_tensor(dst, view(t1[j % 2])[r], view(sh[j % 2])[r], ALU.add)
                        last.then_inc(st.qk_out, 1)
                        pool.wait_ge(st.qk_out, B * st.NQK + j + 1)
                elif j == 1:
                    pool.wait_ge(st.qk_raw, B * 2 + 2)
                    for m in (0, 1):
                        last = g.tensor_tensor(
                            kv[:, 8 * m:8 * m + 8, :],
                            ksb[:, m, 0:st.NK].unsqueeze(1).to_broadcast([P, 8, st.NK]),
                            headmask[:, :].unsqueeze(2).to_broadcast([P, 8, st.NK]), ALU.mult)
                    last.then_inc(st.qk_out, 1)

            for st in stages:
                if st.index:
                    pool.wait_ge(stages[st.index - 1].y_ready, stages[st.index - 1].b0 + NB)
                if st.index in (1, 3, 4):
                    g.memset(kbd[:, :, :], 0.0).then_inc(ident_step, 1)
                    g.memset(vaug[:, :], 1.0).then_inc(v_ones, 1)
                    pool.wait_ge(ident_step, 7 + (1, 3, 4).index(st.index) + 1)

                def run(t, steps):
                    for what, j in steps:
                        if what == "LN":
                            norm_rstd(st, t, 0)
                        elif what == "CN" and st.rope:
                            ctx_rstd_(st, t)
                        elif what == "QK":
                            finish_qk(st, t, j)

                walk(pool, st, run)

        @block.scalar
        def _(act):
            a = nc.scalar
            act.wait_ge(param_in, 64)
            a.activation(esb[:, :, :], condsb[:, :, :], ACT.Exp, scale=-1.0).then_inc(silu_step, 1)
            a.activation(bq4[:, :], colsb[:, COLS["b_qk"]:COLS["b_qk"] + 2], ACT.Copy, scale=0.25)\
                .then_inc(silu_step, 1)
            act.wait_ge(silu_step, 2)

            def col(name, c, rows_=P):
                return colsb[0:rows_, COLS[name] + c:COLS[name] + c + 1]

            for st in stages:
                if st.index:
                    act.wait_ge(stages[st.index - 1].y_ready, stages[st.index - 1].b0 + NB)
                if st.att:
                    act.wait_ge(v_ones, 1 + (0, 1, None, 2, 3)[st.index])

                def run(t, steps):
                    B = t.B
                    nxt = B + 1
                    for what, j in steps:
                        if what in JOBS:
                            k, before, jobs = t.slot()
                            ps = ps_j[k]
                            pv = ps[:, :].rearrange("p (m n) -> p m n", m=2)
                        if what == "LNT":
                            act.wait_ge(st.pj_ready, jobs)
                            turn = t.i + t.par if t.real else t.i
                            act.wait_ge(st.x_in[1 - t.par], st.loads * (turn + 1))
                            c = coef[1 - t.par]
                            a.activation(hT[:, 0, :], pv[:, 0, :], ACT.Identity, scale=c[:, 0:1], bias=c[:, 2:3])
                            a.activation(hT[:, 1, :], pv[:, 1, :], ACT.Identity, scale=c[:, 1:2], bias=c[:, 3:4])\
                                .then_inc(st.h_ready, 1)
                            act.wait_ge(st.h_ready, nxt + 1)
                            act.sem_inc(st.pj_free[k], 1)
                        elif what == "CT":
                            act.wait_ge(st.pj_ready, jobs)
                            if st.rope:
                                a.activation(cT[:, 0, :], ps[:, 0:NC], ACT.Identity, scale=col("lnc_w", 0),
                                             bias=col("lnc_b", 0))
                                a.activation(cT[0:64, 1, :], ps[0:64, NC:2 * NC], ACT.Identity,
                                             scale=col("lnc_w", 1, 64), bias=col("lnc_b", 1, 64))\
                                    .then_inc(st.cT_ready, 1)
                                act.wait_ge(st.cT_ready, nxt + 1)
                            else:
                                a.activation(cRaw[:, 0, :], ps[:, 0:NC], ACT.Copy)
                                a.activation(cRaw[0:64, 1, :], ps[0:64, NC:2 * NC], ACT.Copy)\
                                    .then_inc(st.c_raw, 1)
                                act.wait_ge(st.c_raw, nxt + 1)
                            act.sem_inc(st.pj_free[k], 1)
                        elif what == "CP":
                            act.wait_ge(st.pj_ready, jobs)
                            for m in (0, 1):
                                last = a.activation(cT[:, m, :], ps[:, m * NC:m * NC + NC], ACT.Identity,
                                                    bias=col("b_ctx", m))
                            last.then_inc(st.cT_ready, 1)
                            act.wait_ge(st.cT_ready, nxt + 1)
                            act.sem_inc(st.pj_free[k], 1)
                        elif what == "QK" and not st.rope:
                            act.wait_ge(st.pj_ready, jobs)
                            for m in (0, 1):
                                if j == 0:
                                    last = a.activation(qT[:, m, :], pv[:, m, :], ACT.Identity, scale=0.25,
                                                        bias=0.0 if st.cross else bq4[:, m:m + 1])
                                else:
                                    if m == 0:
                                        act.wait_ge(st.qk_out, nxt)
                                    last = a.activation(ksb[:, m, 0:st.NK], ps[:, m * st.NK:(m + 1) * st.NK],
                                                        ACT.Identity, bias=0.0 if st.cross else col("b_qk", 2 + m))
                            last.then_inc(st.qk_raw, 1)
                            act.wait_ge(st.qk_raw, nxt * 2 + j + 1)
                            act.sem_inc(st.pj_free[k], 1)
                        elif what == "V" and (st.DH == 64 or st.cross):
                            act.wait_ge(st.pj_ready, jobs)
                            if st.DH == 64:
                                dst = vview(st)[0:st.KP, j // 2, 8 * (j % 2):8 * (j % 2) + 8, 0:64]
                                src = ps[0:st.KP, :].rearrange("p (h d) -> p h d", h=8)
                            else:
                                dst = vview(st)[0:st.KP, 0, :, 0:16]
                                src = ps[0:st.KP, 0:256].rearrange("p (h d) -> p h d", h=H)
                            a.activation(dst, src, ACT.Copy).then_inc(st.v_ready, 1)
                            act.wait_ge(st.v_ready, B * st.NV + j + 1)
                            act.sem_inc(st.pj_free[k], 1)
                        elif what == "S":
                            act.wait_ge(st.max_ready, B * st.U + j + 1)
                            if j >= 2:
                                act.wait_ge(st.pt_ready, B * st.U + j - 1)
                            for hh in range(st.HU):
                                c = slice(hh * st.NK, (hh + 1) * st.NK)
                                last = a.activation(prob[j % 2][:, c], ps_s[j % 2][:, c], ACT.Exp,
                                                    bias=negmax[j % 2][:, hh:hh + 1])
                            last.then_inc(st.p_ready, 1)
                        elif what == "OT":
                            act.wait_ge(st.pj_ready, jobs)
                            g_, tt = j // TT, j % TT
                            a.activation(oT[:, 2 * g_:2 * g_ + 2, tt * P:tt * P + P],
                                         ps[:, 0:256].rearrange("p (f n) -> p f n", f=2), ACT.Copy)\
                                .then_inc(st.oT_done, 1)
                            act.wait_ge(st.oT_done, B * st.NO + j + 1)
                            act.sem_inc(st.pj_free[k], 1)
                        elif what == "F1":
                            act.wait_ge(st.pj_ready, jobs)
                            name = "ff_b1" if st.index == 2 else "b_fc1"
                            for m in (0, 1):
                                last = a.activation(oT[:, 2 * j + m, :], pv[:, m, :], st.gelu,
                                                    bias=col(name, 2 * j + m))
                            last.then_inc(st.g_ready, 1)
                            act.wait_ge(st.g_ready, B * 4 + j + 1)
                            act.sem_inc(st.pj_free[k], 1)

                walk(act, st, run)

        @block.vector
        def _(dve):
            v = nc.vector
            dve.wait_ge(silu_step, 2)
            v.tensor_scalar(esb[:, :, :], esb[:, :, :], 1.0, None, ALU.add).then_inc(mod_step, 1)
            dve.wait_ge(mod_step, 1)
            v.reciprocal(esb[:, :, :], esb[:, :, :]).then_inc(mod_step, 1)
            dve.wait_ge(mod_step, 2)
            v.tensor_tensor(silub[:, :, :], esb[:, :, :], condsb[:, :, :], ALU.mult).then_inc(mod_step, 1)
            dve.wait_ge(mod_mm, 1)
            bias_at = [COLS["g1_b"] + c for c in range(8)] + [COLS["b_ada"] + c for c in range(12)]
            gains = (0, 1, 4, 5, 10, 11, 14, 15, 18, 19)
            for c, at in enumerate(bias_at):
                last = v.tensor_scalar(modsb[:, c, :], ps_j[0][:, c * NB:(c + 1) * NB], colsb[:, at:at + 1],
                                       1.0 if c in gains else 0.0, ALU.add, ALU.add)
            last.then_inc(mod_step, 1)
            dve.wait_ge(mod_step, 4)
            for s in range(5):
                for k in range(KD):
                    if s < 2:
                        w = colsb[:, COLS[("ln1_w", "ln2_w")[s]] + k:COLS[("ln1_w", "ln2_w")[s]] + k + 1]
                        b_ = colsb[:, COLS[("ln1_b", "ln2_b")[s]] + k:COLS[("ln1_b", "ln2_b")[s]] + k + 1]
                        gain, shift = modsb[:, 4 * s + k, :], modsb[:, 4 * s + 2 + k, :]
                        v.tensor_scalar(coefsb[:, s, :, k], gain, w, None, ALU.mult)
                        last = v.scalar_tensor_tensor(coefsb[:, s, :, 2 + k], gain, b_, shift, ALU.mult, ALU.add)
                    else:
                        c = 8 + 4 * (s - 2)
                        v.tensor_copy(coefsb[:, s, :, k], modsb[:, c + 2 + k, :])
                        last = v.tensor_copy(coefsb[:, s, :, 2 + k], modsb[:, c + k, :])
            last.then_inc(coef_ready, 1)
            dve.wait_ge(param_in, 64)
            dve.wait_ge(ident_step, 7)

            for st in stages:
                if st.att:
                    dve.wait_ge(v_ones, 1 + (0, 1, None, 2, 3)[st.index])
                norms = 1 + st.cross * st.rope
                outs = st.NO if st.att else 0

                def norm(t):
                    B = t.B + 1
                    par = 1 - t.par
                    turn = t.i + t.par if t.real else t.i
                    dve.wait_ge(st.x_in[par], st.loads * (turn + 1))
                    for tt in range(TT):
                        last = v.bn_stats(stats[:, tt, :], xt[par][:, tt, :])
                    last.then_inc(st.dve_step, 1)
                    dve.wait_ge(st.dve_step, B * norms + (t.B * outs if t.real else 0) + 1)
                    v.memset(tick[:, :], 0.0)
                    for tt in range(TT):
                        last = v.bn_aggr(mv[:, tt, :], stats[:, tt, :])
                    last.then_inc(st.ln_sums, 1)
                    dve.wait_ge(st.ln_rstd, B + 1)
                    dve.wait_ge(st.h_ready, B)
                    for tt in range(TT):
                        last = v.tensor_scalar(xhat[:, tt, :], xt[par][:, tt, :], mv[:, tt, 0:1],
                                               rstd[:, tt:tt + 1], ALU.subtract, ALU.mult)
                    last.then_inc(st.xhat_ready, 1)

                def norm_ctx(t):
                    B = t.B + 1
                    par = 1 - t.par
                    turn = t.i + t.par if t.real else t.i
                    dve.wait_ge(st.x_in[par], st.loads * (turn + 1))
                    dve.wait_ge(st.cT_ready, B)
                    if st.rope:
                        v.bn_stats(cstats[0:NC, :], ctxt[par][0:NC, :]).then_inc(st.dve_step, 1)
                        dve.wait_ge(st.dve_step, B * norms + (t.B * outs if t.real else 0) + 2)
                        v.memset(tick[:, :], 0.0)
                        v.bn_aggr(cmv[0:NC, :], cstats[0:NC, :]).then_inc(st.ctx_sums, 1)
                        dve.wait_ge(st.ctx_rstd, B + 1)
                        v.tensor_scalar(chat[0:NC, :], ctxt[par][0:NC, :], cmv[0:NC, 0:1], crstd[0:NC, 0:1],
                                        ALU.subtract, ALU.mult).then_inc(st.chat_ready, 1)
                    else:
                        v.tensor_copy(chat[0:NC, :], ctxt[par][0:NC, :]).then_inc(st.chat_ready, 1)

                def run(t, steps):
                    B = t.B
                    nxt = B + 1
                    for what, j in steps:
                        if what in JOBS:
                            k, before, jobs = t.slot()
                            ps = ps_j[k]
                        if what == "LN":
                            norm(t)
                        elif what == "CN":
                            norm_ctx(t)
                        elif what == "QK" and st.rope:
                            half = st.NQK // 2
                            isk = j >= half
                            n = st.NK if isk else N
                            dve.wait_ge(st.pj_ready, jobs)
                            if j >= 2:
                                dve.wait_ge(st.qk_out, nxt * st.NQK + j - 1)
                            cos = ropesb[:, 2 if isk else 0, 0:n].unsqueeze(1).to_broadcast([P, 2, n])
                            v.tensor_tensor(t1[j % 2][:, 0:2 * n].rearrange("p (m n) -> p m n", m=2),
                                            ps[:, 0:2 * n].rearrange("p (m n) -> p m n", m=2), cos, ALU.mult)
                            v.stream_shuffle(sh[j % 2][:, 0:2 * n], ps[:, 0:2 * n], [c ^ 1 for c in range(32)])\
                                .then_inc(st.qk_raw, 1)
                            dve.wait_ge(st.qk_raw, nxt * st.NQK + j + 1)
                            dve.sem_inc(st.pj_free[k], 1)
                        elif what == "V" and st.DH == 16 and not st.cross:
                            dve.wait_ge(st.pj_ready, jobs)
                            src = ps[:, :].rearrange("p (t h d) -> p t h d", t=TT, h=H)
                            bv = rowsb[:, 6, :].rearrange("p (h d) -> p h d", h=H)
                            for tt in range(TT):
                                last = v.tensor_tensor(vview(st)[:, tt, :, 0:16], src[:, tt], bv, ALU.add)
                            last.then_inc(st.v_ready, 1)
                            dve.wait_ge(st.v_ready, B + 1)
                            dve.sem_inc(st.pj_free[k], 1)
                        elif what == "S":
                            dve.wait_ge(st.s_ready, B * st.U + j + 1)
                            if j >= 2:
                                dve.wait_ge(st.p_ready, B * st.U + j - 1)
                            v.tensor_reduce(negmax[j % 2][:, 0:st.HU],
                                            ps_s[j % 2][:, 0:st.HU * st.NK].rearrange("p (h n) -> p h n", h=st.HU),
                                            AX_X, ALU.max, negate=True).then_inc(st.max_ready, 1)
                        elif what == "T":
                            dve.wait_ge(st.pt_ready, B * st.U + j + 1)
                            if j >= 2:
                                dve.wait_ge(st.av_done, B * st.U + j - 1)
                            v.tensor_copy(probT[j % 2][0:st.KP, :], ps_t[j % 2][0:st.KP, :])\
                                .then_inc(st.pt_copied, 1)
                        elif what == "AV" and j % st.UI == st.UI - 1:
                            n = j // st.UI
                            dve.wait_ge(st.av_done, B * st.U + j + 1)
                            w = st.DH + 1
                            o = ps_o[n % 2][:, 0:st.HG * w].rearrange("p (h d) -> p h d", h=st.HG)
                            v.reciprocal(rinv[n % 2][:, 0:st.HG], o[:, :, st.DH]).then_inc(st.dve_step, 1)
                            t.seen += 1
                            dve.wait_ge(st.dve_step, t.step_base + t.seen)
                            if n >= 2:
                                dve.wait_ge(st.oT_done, B * st.NO + n - 1)
                            v.tensor_tensor(osb[n % 2][:, :].rearrange("p (h d) -> p h d", h=st.HG),
                                            o[:, :, 0:st.DH],
                                            rinv[n % 2][:, 0:st.HG].unsqueeze(2).to_broadcast([P, st.HG, st.DH]),
                                            ALU.mult).then_inc(st.o_ready, 1)
                        elif what == "WO":
                            dve.wait_ge(st.pj_ready, jobs)
                            dve.wait_ge(st.xb_ready, B + 1)
                            if True:
                                dve.wait_ge(st.stored[t.par], 16 * t.i + 1)
                            v.tensor_tensor(yt[t.par][:, :, :], ps[:, :].rearrange("p (t d) -> p t d", t=TT),
                                            xb[t.par][:, :, :], ALU.add).then_inc(st.y_ready, 1)
                            dve.wait_ge(st.y_ready, B + 1)
                            dve.sem_inc(st.pj_free[k], 1)

                def run_counted(t, steps):
                    if t.real:
                        has_next = any(w == "LN" for w, _ in steps)
                        t.step_base = t.B * outs + (t.B + 1 + has_next) * norms
                    t.seen = 0
                    run(t, steps)

                walk(dve, st, run_counted)

        @block.tensor
        def _(pe):
            te = nc.tensor
            pe.wait_ge(param_in, 64)
            pe.wait_ge(mod_w_in, 16 * len(weights["mod"]))
            pe.wait_ge(mod_step, 3)
            tile = 0
            for name, k_, n_, at, _src in weights["mod"]:
                w = mod_w[:, at:at + k_ * n_].rearrange("p (k n) -> p k n", k=k_)
                src = silub if name == "W_ada" else condsb
                for m in range(n_ // P):
                    for k in range(KD):
                        last = te.matmul(ps_j[0][:, tile * NB:(tile + 1) * NB], w[:, k, m * P:(m + 1) * P],
                                         src[:, k, :], start=(k == 0), stop=(k == KD - 1))
                    tile += 1
            last.then_inc(mod_mm, 1)
            pe.wait_ge(coef_ready, 1)
            pe.wait_ge(ident_step, 7)
            for st in stages[0:5]:
                for k in (0, 1):
                    pe.sem_inc(st.pj_free[k], 1)

            for st in stages:
                if st.index:
                    pe.wait_ge(stages[st.index - 1].y_ready, stages[st.index - 1].b0 + NB)
                nw = sum(1 + (src.shape[0] % P != 0) for src, *_ in weights[st.index].values())
                pe.wait_ge(st.weights_in, 16 * nw * (2 if st.b0 else 1))

                def project(ps_out, lhsT, rhs, rows_):
                    for k, r in enumerate(rows_):
                        last = te.matmul(ps_out, lhsT(k, r), rhs(k, r), start=(k == 0), stop=(k == len(rows_) - 1))
                    return last

                def run(t, steps):
                    B = t.B
                    nxt = B + 1
                    for what, j in steps:
                        if what in JOBS:
                            k_, before, jobs = t.slot()
                            ps = ps_j[k_]
                            pv = ps[:, :].rearrange("p (m n) -> p m n", m=2)
                            pe.wait_ge(st.pj_free[k_], before + 1)
                        if what == "LNT":
                            pe.wait_ge(st.xhat_ready, nxt + 1)
                            for f in range(KD):
                                for tt in range(TT):
                                    last = te.transpose(pv[:, f, tt * P:(tt + 1) * P],
                                                        xhat[:, tt, f * P:(f + 1) * P], ident[:, :])
                        elif what == "CT":
                            pe.wait_ge(st.chat_ready, nxt + 1)
                            te.transpose(ps[:, 0:NC], chat[0:NC, 0:P], ident[0:NC, 0:NC])
                            last = te.transpose(ps[0:64, NC:2 * NC], chat[0:NC, P:DC], ident[0:NC, 0:NC])
                        elif what == "CP":
                            pe.wait_ge(st.c_raw, nxt + 1)
                            w = wview(st, "wctx")
                            for m in (0, 1):
                                last = project(ps[:, m * NC:(m + 1) * NC],
                                               lambda k, r: w[0:r, k, m * P:(m + 1) * P],
                                               lambda k, r: cRaw[0:r, k, :], (P, DC - P))
                        elif what == "QK":
                            half = st.NQK // 2
                            isk = j >= half
                            if j == 0:
                                pe.wait_ge(st.h_ready, nxt + 1)
                            if j == half and st.cross:
                                pe.wait_ge(st.cT_ready, nxt + 1)
                            w = wview(st, "wk" if isk else "wq")
                            n = st.NK if isk else N
                            src = cT if isk and st.cross else hT
                            rows_ = (P, DC - P) if isk and st.cross and st.rope else (P, P)
                            for mm in (0, 1):
                                m = 2 * (j % half) + mm
                                last = project(ps[:, mm * n:(mm + 1) * n],
                                               lambda k, r: w[0:r, k, m * P:(m + 1) * P],
                                               lambda k, r: src[0:r, k, 0:n], rows_)
                        elif what == "V":
                            w = wview(st, "wv")
                            src = cT if st.cross else hT
                            rows_ = (P, DC - P) if st.cross and st.rope else (P, P)
                            if st.DH == 64:
                                tt, hf = j // 2, j % 2
                                last = project(ps[0:st.KP, :],
                                               lambda k, r: src[0:r, k, tt * P:tt * P + st.KP],
                                               lambda k, r: w[0:r, k, hf * 512:(hf + 1) * 512], rows_)
                            else:
                                for tt in range(st.KT):
                                    last = project(ps[0:st.KP, tt * 256:(tt + 1) * 256],
                                                   lambda k, r: src[0:r, k, tt * P:tt * P + st.KP],
                                                   lambda k, r: w[0:r, k, :], rows_)
                        elif what == "S":
                            if j == 0:
                                if st.rope:
                                    pe.wait_ge(st.qk_out, (B + 1) * st.NQK)
                                else:
                                    pe.wait_ge(st.qk_raw, (B + 1) * 2)
                                    pe.wait_ge(st.qk_out, B + 1)
                            if j >= 2:
                                pe.wait_ge(st.p_ready, B * st.U + j - 1)
                            grp, rest = j // (TT * st.UI), j % (TT * st.UI)
                            tt, h0 = rest // st.UI, grp * st.HG + (rest % st.UI) * st.HU
                            kv = kview(st)
                            step = min(st.HU, st.TH)
                            for h in range(h0, h0 + st.HU, step):
                                c = (h - h0) * st.NK
                                last = te.matmul(ps_s[j % 2][:, c:c + step * st.NK],
                                                 qT[:, h // st.TH, tt * P:(tt + 1) * P],
                                                 kv[:, h:h + step, :], start=True, stop=True)
                            last.then_inc(st.s_ready, 1)
                        elif what == "T":
                            pe.wait_ge(st.p_ready, B * st.U + j + 1)
                            if j >= 2:
                                pe.wait_ge(st.pt_copied, B * st.U + j - 1)
                            for blk in range(4):
                                last = te.transpose(ps_t[j % 2][0:st.KP, blk * P:(blk + 1) * P],
                                                    prob[j % 2][:, blk * st.KP:(blk + 1) * st.KP], ident[:, :])
                            last.then_inc(st.pt_ready, 1)
                        elif what == "AV":
                            if j == 0:
                                pe.wait_ge(st.v_ready, (B + 1) * st.NV)
                            pe.wait_ge(st.pt_copied, B * st.U + j + 1)
                            n = j // st.UI
                            if j % st.UI == 0:
                                if n >= 2:
                                    pe.wait_ge(st.o_ready, B * st.NO + n - 1)
                            grp, rest = j // (TT * st.UI), j % (TT * st.UI)
                            w = st.DH + 1
                            for hh in range(st.HU):
                                pos = (rest % st.UI) * st.HU + hh
                                for kt in range(st.KT):
                                    blk = hh * st.KT + kt
                                    last = te.matmul(ps_o[n % 2][:, pos * w:(pos + 1) * w],
                                                     probT[j % 2][0:st.KP, blk * P:(blk + 1) * P],
                                                     vview(st)[0:st.KP, kt, grp * st.HG + pos, :],
                                                     start=(kt == 0), stop=(kt == st.KT - 1))
                            last.then_inc(st.av_done, 1)
                        elif what == "OT":
                            pe.wait_ge(st.o_ready, B * st.NO + j + 1)
                            for f in (0, 1):
                                last = te.transpose(ps[:, f * P:(f + 1) * P], osb[j % 2][:, f * P:(f + 1) * P],
                                                    ident[:, :])
                        elif what == "F1":
                            if j == 0:
                                pe.wait_ge(st.h_ready, B + 1)
                            w = wview(st, "w1")
                            for mm in (0, 1):
                                m = 2 * j + mm
                                last = project(pv[:, mm, :], lambda k, r: w[:, k, m * P:(m + 1) * P],
                                               lambda k, r: hT[:, k, :], (P, P))
                        elif what == "WO":
                            w = wview(st, "wo")
                            if st.att:
                                pe.wait_ge(st.oT_done, (B + 1) * st.NO)
                                kt_n = st.M
                            else:
                                pe.wait_ge(st.g_ready, (B + 1) * 4)
                                kt_n = 8
                            for tt in range(TT):
                                last = project(pv[:, tt, :], lambda k, r: oT[:, k, tt * P:(tt + 1) * P],
                                               lambda k, r: w[:, k, :], (P,) * kt_n)
                        if what in JOBS:
                            last.then_inc(st.pj_ready, 1)

                walk(pe, st, run)


def kernel(**inputs):
    import concourse.bacc as _bacc
    from concourse import mybir as _mybir
    from concourse.bass_utils import run_bass_kernel_spmd as _run

    nc = _bacc.Bacc("TRN2", target_bir_lowering=False, num_devices=1)
    arrays = {}

    def dram(name, a):
        a = np.ascontiguousarray(a)
        arrays[name] = a
        return nc.dram_tensor(name, a.shape, _mybir.dt.from_np(a.dtype), kind="ExternalInput").ap()

    L0, L1 = "L0_xcond_", "L1_xcond_"
    g = {k: np.asarray(v) for k, v in inputs.items()}

    def columns(v):
        v = np.concatenate([v, np.zeros((-len(v)) % P, v.dtype)])
        return v.reshape(-1, P).T

    qkv_b = g[L1 + "b_qkv"]
    order = [g[L0 + "ln1_w"], g[L0 + "ln1_b"], g[L0 + "ln2_w"], g[L0 + "ln2_b"], g[L0 + "g1_b"], g[L0 + "b1_b"],
             g[L0 + "g2_b"], g[L0 + "b2_b"], g[L0 + "ca_lnc_w"], g[L0 + "ca_lnc_b"], g[L0 + "ff_b1"],
             g[L1 + "b_ada"], qkv_b[0:2 * D], g[L1 + "b_ctx"], g[L1 + "b_fc1"]]
    cols = dram("in_cols", np.concatenate([columns(v) for v in order], axis=1))
    condT = dram("in_condT", g["cond_1024"].reshape(NB, KD, P).transpose(2, 1, 0))
    rows = dram("in_rows", np.stack([g[L0 + "sa_bo"], g[L0 + "ca_bo"], g[L0 + "ff_b2"], g[L1 + "b_proj"],
                                     g[L1 + "b_out"], g[L1 + "b_fc2"], qkv_b[2 * D:3 * D]]))

    f32 = np.float32
    inv = (f32(1.0) / np.power(f32(10000.0), np.arange(0, 64, 2, dtype=f32) / f32(64))).astype(f32)
    ang = (np.arange(N, dtype=f32)[:, None] * inv[None, :]).astype(f32)
    sin, cos = np.sin(ang.astype(np.float64)), np.cos(ang.astype(np.float64))
    freq = (np.arange(P) % 64) // 2
    sign = np.where(np.arange(P) % 2 == 0, -1.0, 1.0)[:, None]
    c, s = cos.T[freq], sin.T[freq] * sign
    ropes = dram("in_ropes", np.stack([c * 0.125, s * 0.125, c, s], axis=1).astype(f32))

    def w(name):
        return dram("in_" + name, g[name])

    def place(*items):
        out, at = {}, 0
        for name, src, n in items:
            k = -(-src.shape[0] // P)
            out[name] = (src, k, n, at)
            at += k * n
        return out

    sakv, cakv, qkv = w(L0 + "sa_wkv"), w(L0 + "ca_wkv"), w(L1 + "W_qkv")
    weights = {
        0: place(("wq", w(L0 + "sa_wq"), 1024), ("wk", sakv[:, 0:1024], 1024), ("wv", sakv[:, 1024:2048], 1024),
                 ("wo", w(L0 + "sa_wo"), 256)),
        1: place(("wq", w(L0 + "ca_wq"), 1024), ("wk", cakv[:, 0:1024], 1024), ("wv", cakv[:, 1024:2048], 1024),
                 ("wo", w(L0 + "ca_wo"), 256)),
        2: place(("w1", w(L0 + "ff_w1"), 1024), ("wo", w(L0 + "ff_w2"), 256)),
        3: place(("wq", qkv[:, 0:256], 256), ("wk", qkv[:, 256:512], 256), ("wv", qkv[:, 512:768], 256),
                 ("wo", w(L1 + "W_proj"), 256)),
        4: place(("wctx", w(L1 + "W_ctx"), 256), ("wq", w(L1 + "W_q"), 256), ("wk", w(L1 + "W_k"), 256),
                 ("wv", w(L1 + "W_v"), 256), ("wo", w(L1 + "W_out"), 256)),
        5: place(("w1", w(L1 + "W_fc1"), 1024), ("wo", w(L1 + "W_fc2"), 256)),
    }
    mod, at = [], 0
    for name in ("g1_w", "b1_w", "g2_w", "b2_w", "W_ada"):
        src = w((L1 if name == "W_ada" else L0) + name)
        mod.append((name, KD, src.shape[1], at, src))
        at += KD * src.shape[1]
    weights["mod"] = mod
    x = dram("in_x", g["x"])
    context = dram("in_ctx", g["ctx_768"])
    out = nc.dram_tensor("out_0", [NB, N, D], _mybir.dt.float32, kind="ExternalOutput").ap()
    build(nc, x, context, condT, cols, ropes, rows, weights, out)
    r = _run(nc, [arrays], core_ids=[0])
    return r.results[0]["out_0"]
```

```python
from contextlib import ExitStack

import numpy as np

import concourse.bass as bass
from concourse import mybir

F32 = mybir.dt.float32
F16 = mybir.dt.float16
ALU = mybir.AluOpType
ACT = mybir.ActivationFunctionType
AX_X = mybir.AxisListType.X

P = 128
NB, N, D = 8, 256, 256
KD = D // P
TT = N // P
H = 16
NC, DC = 120, 192
TURNS = NB // 2

HI, LO = 0, 1
PARTS = ((HI, HI), (HI, LO), (LO, HI))
W_SCALE = 64.0
P_SCALE = 1024.0
CHUNK = 1024

COLS = {}


def _columns():
    at = 0
    for name, c in (("ln1_w", 2), ("ln1_b", 2), ("ln2_w", 2), ("ln2_b", 2), ("g1_b", 2), ("b1_b", 2),
                    ("g2_b", 2), ("b2_b", 2), ("lnc_w", 2), ("lnc_b", 2), ("ff_b1", 8), ("b_ada", 12),
                    ("b_qk", 4), ("b_ctx", 2), ("b_fc1", 8)):
        COLS[name] = at
        at += c
    return at


NCOLS = _columns()


class Stage:

    def __init__(self, nc, ctx, index, name, kind, coef, eps, DH=0, cross=False, rope=False, gelu=None, order=0):
        self.index, self.name, self.kind, self.coef, self.eps = index, name, kind, coef, eps
        self.cross, self.rope, self.gelu, self.order = cross, rope, gelu, order
        self.att = kind == "att"

        def sem(what):
            return ctx.enter_context(nc.semaphore(f"{name}_{what}"))

        if self.att:
            self.DH = DH
            self.NK = NC if cross else N
            self.KP = NC if cross else P
            self.KT = self.NK // self.KP
            self.TH = P // DH
            self.M = H * DH // P
            self.HU = 4 if cross else 2
            self.HG = 256 // DH
            self.NG = H // self.HG
            self.UI = self.HG // self.HU
            self.U = self.NG * TT * self.UI
            self.NO = self.NG * TT
            self.NQK = self.M
            self.NV = (2 * self.KT) if DH == 64 else 1
            self.s_ready = sem("s_ready")
            self.max_ready = sem("max_ready")
            self.p_ready = sem("p_ready")
            self.pt_ready = sem("pt_ready")
            self.pt_hi = sem("pt_hi")
            self.pt_copied = sem("pt_copied")
            self.av_done = sem("av_done")
            self.rinv_ready = sem("rinv_ready")
            self.o_ready = sem("o_ready")
            self.oT_hi = sem("oT_hi")
            self.oT_done = sem("oT_done")
            self.v_hi = sem("v_hi")
            self.v_ready = sem("v_ready")
            self.vbias = DH == 16 and not cross
            if self.vbias:
                self.v_raw = sem("v_raw")
            self.qk_raw = sem("qk_raw")
            self.qk_out = sem("qk_out")
            if rope:
                self.rope_step = sem("rope_step")
            if cross:
                self.ctx_in = [sem(f"ctx_in{k}") for k in (0, 1)]
                self.chat_ready = sem("chat_ready")
                self.c_f32 = sem("c_f32")
                self.c_hi = sem("c_hi")
                self.cT_ready = sem("cT_ready")
                if rope:
                    self.ctx_stats = sem("ctx_stats")
                    self.ctx_sums = sem("ctx_sums")
                    self.ctx_veps = sem("ctx_veps")
                    self.ctx_rstd = sem("ctx_rstd")
                else:
                    self.c_raw = sem("c_raw")
        else:
            self.g_f32 = sem("g_f32")
            self.g_hi = sem("g_hi")
            self.g_ready = sem("g_ready")

    def norms(self):
        return ["LN"] + ["CN"] * self.cross

    def turned(self):
        return [("LNT", 0)] + [("CT", 0)] * self.cross + [("CP", 0)] * (self.cross and not self.rope)

    def projections(self):
        return [("QK", j) for j in range(self.NQK)] + [("V", j) for j in range(self.NV)] if self.att else []

    def first_steps(self):
        return [("next", "W", (self, c)) for c in range(self.chunks)] + [
            ("next", w, j) for w, j in [(w, 0) for w in self.norms()] + self.turned() + self.projections()]

    def steps(self, nxt, heavy=None):
        split = [("own", "W", (heavy, c)) for c in range(heavy.chunks)] if heavy else []
        side = [("next", w, j) for w, j in nxt.turned() + nxt.projections()] if nxt else []
        norms = [("next", w, 0) for w in nxt.norms()] if nxt else []
        out = []
        if not self.att:
            return norms + [("own", "F1", j) for j in range(4)] + side + [("own", "WO", 0)] + split
        due = []
        last_step = self.U + 6
        sent = 0
        for n in range(last_step):
            if n < self.U:
                out.append(("own", "S", n))
            if 0 <= n - 2 < self.U:
                out.append(("own", "T", n - 2))
            if n < self.U:
                out.append(("own", "E", n))
            while due and due[0][0] <= n:
                out.append(("own", "OT", due.pop(0)[1]))
            if 0 <= n - 4 < self.U:
                out.append(("own", "AV", n - 4))
                if (n - 4) % self.UI == self.UI - 1:
                    due.append((n + 2, (n - 4) // self.UI))
            if n == 0:
                out += norms
            if split and 2 <= n:
                out.append(split.pop(0))
            want = len(side) if n == last_step - 1 else max(0, (n - 2) * len(side) // (last_step - 2))
            while sent < min(want, len(side)):
                out.append(side[sent])
                sent += 1
        out += [("own", "OT", n) for _, n in due]
        return out + [("own", "WO", 0)] + split


JOBS = ("LNT", "CT", "CP", "QK", "V", "OT", "F1", "WO")


def count_jobs(steps):
    return sum(s[1] in JOBS for s in steps)


def build(nc, x_dram, ctx_dram, condT, cols, ropes, rows, weights, out):
    with ExitStack() as ctx:
        def sb(name, shape, dtype=F32):
            return ctx.enter_context(nc.sbuf_tensor(name, shape, dtype))

        def sem(name):
            return ctx.enter_context(nc.semaphore(name))

        stages = [
            Stage(nc, ctx, 0, "sa0", "att", 0, 1e-5, DH=64, rope=True, order=0),
            Stage(nc, ctx, 1, "ca0", "att", 0, 1e-5, DH=64, cross=True, rope=True, order=1),
            Stage(nc, ctx, 2, "ff0", "ffn", 1, 1e-5, gelu=ACT.Gelu),
            Stage(nc, ctx, 3, "sa1", "att", 2, 1e-6, DH=16, order=2),
            Stage(nc, ctx, 4, "ca1", "att", 3, 1e-6, DH=16, cross=True, order=3),
            Stage(nc, ctx, 5, "ff1", "ffn", 4, 1e-6, gelu=ACT.Gelu_apprx_tanh),
        ]

        xs = [x_dram] + [nc.dram_tensor(f"x_after_{st.name}", [NB, N, D], F32, kind="Internal").ap()
                       for st in stages[:-1]] + [out]
        coef_dram = nc.dram_tensor("coefs", [5, NB, P, 4], F32, kind="Internal").ap()

        WSIZE = 8192
        wsplit = [sb(f"wsplit{k}", [P, 2, WSIZE], F16) for k in (0, 1)]
        wload = [sb(f"wload{k}", [P, CHUNK]) for k in (0, 1)]
        chunks = []
        for st in stages:
            pieces = {}
            for src, k, n, at in weights[st.index].values():
                for kt in range(k):
                    col_, rows_ = at + kt * n, min(P, src.shape[0] - kt * P)
                    pieces.setdefault(col_ // CHUNK, []).append(
                        (col_ % CHUNK, rows_, n, src[kt * P:kt * P + rows_, :]))
            chunks.append([pieces[c] for c in sorted(pieces)])
            st.chunks = len(pieces)
        colsb = sb("colsb", [P, NCOLS])
        condsb = sb("condsb", [P, KD, NB])
        silub = sb("silub", [P, KD, NB])
        esb = sb("esb", [P, KD, NB])
        modsb = sb("modsb", [P, 20, NB])
        coefsb = sb("coefsb", [P, 5, NB, 4])
        ropesb = sb("ropesb", [P, 4, N])
        rowsb = sb("rowsb", [P, 7, D])
        ident = sb("ident", [P, P])
        headmask = sb("headmask", [P, 8])
        halfpow = sb("halfpow", [P, 2])
        epsb = sb("epsb", [P, 2, TT])
        tick = sb("tick", [P, 1])
        zero = sb("zero", [P, 1])
        bq4 = sb("bq4", [P, 2])

        xt = [sb(f"xt{k}", [P, TT, D]) for k in (0, 1)]
        xb = [sb(f"xb{k}", [P, TT, D]) for k in (0, 1)]
        yt = [sb(f"yt{k}", [P, TT, D]) for k in (0, 1)]
        coef = [sb(f"coef{k}", [P, 4]) for k in (0, 1)]
        ctxt = [sb(f"ctxt{k}", [P, DC]) for k in (0, 1)]
        chat = sb("chat", [P, DC])
        c32 = sb("c32", [P, 2, NC])
        cT = sb("cT", [P, 2, 2, NC], F16)
        cRaw = sb("cRaw", [P, 2, 2, NC], F16)
        stats = sb("stats", [P, TT, 6])
        mv = sb("mv", [P, TT, 2])
        veps = sb("veps", [P, TT])
        rstd = sb("rstd", [P, TT])
        cstats = sb("cstats", [P, 6])
        cmv = sb("cmv", [P, 2])
        cveps = sb("cveps", [P, 1])
        crstd = sb("crstd", [P, 1])
        xhat = sb("xhat", [P, TT, D])
        h32 = sb("h32", [P, KD, N])
        hT = sb("hT", [P, 2, KD, N], F16)
        qT = [sb(f"qT{k}", [P, 8, N]) for k in (0, 1)]
        kbd = [sb(f"kbd{k}", [P, H, N]) for k in (0, 1)]
        ksb = sb("ksb", [P, 2, N])
        v32 = sb("v32", [P, TT, D])
        vaug = [sb(f"vaug{k}", [P, 2, 2 * H * 65], F16) for k in (0, 1)]
        sh = [sb(f"sh{k}", [P, 2 * N]) for k in (0, 1)]
        t1 = [sb(f"t1_{k}", [P, 2 * N]) for k in (0, 1)]
        negmax = [sb(f"negmax{k}", [P, 4]) for k in (0, 1)]
        prob = [sb(f"prob{k}", [P, 512]) for k in (0, 1)]
        probT = [sb(f"probT{k}", [P, 2, 512], F16) for k in range(4)]
        rinv = [sb(f"rinv{k}", [P, H]) for k in (0, 1)]
        osb = [sb(f"osb{k}", [P, 256]) for k in (0, 1)]
        oT = sb("oT", [P, 2, 8, N], F16)

        def bank(name):
            return ctx.enter_context(nc.psum_tensor(name, [P, 512], F32))

        ps_s = [bank("ps_s0"), bank("ps_s1")]
        ps_t = [bank("ps_t0"), bank("ps_t1")]
        ps_o = [bank("ps_o0"), bank("ps_o1")]
        ps_j = [bank("ps_j0"), bank("ps_j1")]

        param_in = sem("param_in")
        ident_step = sem("ident_step")
        silu_step = sem("silu_step")
        mod_mm = sem("mod_mm")
        mod_step = sem("mod_step")
        coef_out = sem("coef_out")
        coef_ready = sem("coef_ready")
        mod_w_in = sem("mod_w_in")
        kv_blank = sem("kv_blank")
        x_in = [sem(f"x_in{k}") for k in (0, 1)]
        stored = [sem(f"stored{k}") for k in (0, 1)]
        ln_stats = sem("ln_stats")
        ln_sums = sem("ln_sums")
        ln_veps = sem("ln_veps")
        ln_rstd = sem("ln_rstd")
        xhat_ready = sem("xhat_ready")
        xb_ready = sem("xb_ready")
        h_f32 = sem("h_f32")
        h_hi = sem("h_hi")
        h_ready = sem("h_ready")
        w_in = [sem(f"w_in{k}") for k in (0, 1)]
        w_hi = sem("w_hi")
        w_ready = sem("w_ready")
        blank0 = sem("blank0")
        y_ready = sem("y_ready")
        pj_ready = sem("pj_ready")
        pj_free = [sem(f"pj_free{k}") for k in (0, 1)]
        mod_w = {name: kbd[name == "W_ada"][:, :, :].rearrange("p h n -> p (h n)") for name, *_ in weights["mod"]}

        def wview(st, name):
            k, n, at = weights[st.index][name][1:4]
            return wsplit[st.index % 2][:, :, at:at + k * n].rearrange("p s (k n) -> p s k n", k=k)

        def vview(t):
            st = t.st
            return vaug[t.par][:, :, 0:st.KT * H * (st.DH + 1)].rearrange("p s (t h d) -> p s t h d", t=st.KT, h=H)

        def kview(t):
            flat = kbd[t.par][:, :, :].rearrange("p h n -> p (h n)")
            return flat[:, 0:H * t.st.NK].rearrange("p (h n) -> p h n", h=H)

        class Batch:

            def __init__(self, st, i, par):
                self.st, self.i, self.par = st, i, par
                self.B = 2 * i + par
                self.G = 2 * i + (par + NB * st.index)
                self.GP = i + TURNS * st.index

        class Jobs:

            def __init__(self, i, per_turn, at):
                self.i, self.per_turn, self.at = i, per_turn, at

            def slot(self):
                j, self.at = self.at, self.at + 1
                return j % 2, self.i * (self.per_turn // 2) + j // 2, self.i * self.per_turn + j + 1

        def chunks_before(st, c):
            return sum(len(x) for x in chunks[:st.index]) + c

        def loads_before(st, c):
            g = chunks_before(st, c)
            flat = [x for stage_chunks in chunks for x in stage_chunks]
            return sum(len(x) for x in flat[g % 2:g:2])

        def walk(eng, run, enter, begin=None):
            enter(stages[0])
            jobs = Jobs(0, 0, 0)
            run(None, Batch(stages[0], 0, 0), jobs, stages[0].first_steps())
            at = jobs.at
            for s, st in enumerate(stages):
                per = count_jobs(st.steps(st))
                if begin:
                    begin(st)
                with eng.Fori(0, TURNS - 1) as i:
                    run(Batch(st, i, 0), Batch(st, i, 1), Jobs(i, 2 * per, at), st.steps(st))
                    run(Batch(st, i, 1), Batch(st, i + 1, 0), Jobs(i, 2 * per, at + per), st.steps(st))
                at += (NB - 2) * per
                i = TURNS - 1
                nxt = stages[s + 1] if s + 1 < len(stages) else None
                run(Batch(st, i, 0), Batch(st, i, 1), Jobs(0, 0, at), st.steps(st, nxt))
                at += per
                if nxt:
                    enter(nxt)
                run(Batch(st, i, 1), Batch(nxt, 0, 0) if nxt else None, Jobs(0, 0, at), st.steps(nxt))
                at += count_jobs(st.steps(nxt))

        block = ctx.enter_context(nc.Block())

        @block.sync
        def _(sp):
            sp.dma_start(colsb[:, :], cols).then_inc(param_in, 16)
            sp.dma_start(condsb[:, :, :], condT).then_inc(param_in, 16)
            sp.dma_start(ropesb[:, :, :], ropes).then_inc(param_in, 16)
            sp.dma_start(rowsb[:, :, :], rows.partition_broadcast(P)).then_inc(param_in, 16)
            for name, k, n, at, src in weights["mod"]:
                sp.dma_start(mod_w[name][:, at:at + k * n].rearrange("p (k n) -> p k n", k=k),
                             src.rearrange("(k p) n -> p k n", p=P)).then_inc(mod_w_in, 16)

            def load_x(t, b):
                st = t.st
                if not (st.index == 0 and b is t.par):
                    sp.wait_ge(xhat_ready, t.G - 1)
                    sp.wait_ge(xb_ready, t.G - 1)
                    sp.wait_ge(h_ready, t.G - 1)
                if st.index:
                    sp.wait_ge(stored[t.par], 16 * (t.GP - TURNS + 1) + 1)
                sp.dma_start(xt[t.par][:, :, :], xs[st.index][b].rearrange("(t p) d -> p t d", p=P))\
                    .then_inc(x_in[t.par], 16)
                sp.dma_start(coef[t.par][:, :], coef_dram[st.coef, b]).then_inc(x_in[t.par], 16)
                if st.cross:
                    if b is not t.par:
                        sp.wait_ge(st.chat_ready, t.B - 1)
                    sp.dma_start(ctxt[t.par][0:NC, :], ctx_dram[b]).then_inc(st.ctx_in[t.par], 16)

            def store_y(t, b):
                sp.wait_ge(y_ready, t.G + 1)
                sp.dma_start(xs[t.st.index + 1][b].rearrange("(t p) d -> p t d", p=P), yt[t.par][:, :, :])\
                    .then_inc(stored[t.par], 16)

            for par in (0, 1):
                sp.sem_inc(stored[par], 1)
            sp.wait_ge(coef_ready, 1)
            sp.dma_start(coef_dram.rearrange("s b p c -> p s b c"), coefsb[:, :, :, :]).then_inc(coef_out, 16)
            sp.wait_ge(coef_out, 16)
            for par in (0, 1):
                load_x(Batch(stages[0], 0, par), par)
            for s, st in enumerate(stages):
                nxt = stages[s + 1] if s + 1 < len(stages) else None
                with sp.Fori(0, TURNS - 1) as i:
                    for par in (0, 1):
                        load_x(Batch(st, i + 1, par), 2 * i + (2 + par))
                        store_y(Batch(st, i, par), 2 * i + par)
                for par in (0, 1):
                    if nxt:
                        load_x(Batch(nxt, 0, par), par)
                    store_y(Batch(st, TURNS - 1, par), NB - 2 + par)
            for par in (0, 1):
                sp.wait_ge(stored[par], 16 * TURNS * len(stages) + 1)

        @block.gpsimd
        def _(pool):
            g = nc.gpsimd
            g.memset(wload[0][:, :], 0.0)
            g.memset(wload[1][:, :], 0.0).then_inc(blank0, 1)
            g.memset(ident[:, :], 0.0).then_inc(ident_step, 1)
            g.memset(headmask[:, :], 1.0).then_inc(ident_step, 1)
            g.memset(zero[:, :], 0.0)
            g.memset(epsb[:, 0, :], stages[0].eps)
            g.memset(epsb[:, 1, :], stages[3].eps)
            g.memset(halfpow[:, :], -0.5).then_inc(ident_step, 1)
            pool.wait_ge(ident_step, 3)
            g.affine_select(out=ident[:, :], in_=ident[:, :], compare_op=ALU.not_equal, fill=1.0, base=0,
                            pattern=[[-1, P]], channel_multiplier=1).then_inc(ident_step, 1)
            g.affine_select(out=headmask[:, :], in_=headmask[:, :], compare_op=ALU.is_ge, fill=0.0, base=0,
                            pattern=[[-16, 8]], channel_multiplier=1).then_inc(ident_step, 1)
            pool.wait_ge(ident_step, 5)
            g.affine_select(out=headmask[:, :], in_=headmask[:, :], compare_op=ALU.is_ge, fill=0.0, base=15,
                            pattern=[[16, 8]], channel_multiplier=-1).then_inc(ident_step, 1)
            pool.wait_ge(ident_step, 6)

            def blank(st, par):
                t = Batch(st, 0, par)
                g.memset(kbd[par][:, :, :], 0.0)
                for kt in range(st.KT):
                    g.memset(vview(t)[:, HI, kt, :, st.DH], 1.0)
                    last = g.memset(vview(t)[:, LO, kt, :, st.DH], 0.0)
                last.then_inc(kv_blank, 1)
                pool.wait_ge(kv_blank, 2 * st.order + par + 1)

            def enter(st):
                if st.att:
                    if st.index:
                        pool.wait_ge(y_ready, NB * st.index - 1)
                    else:
                        pool.wait_ge(mod_mm, 1)
                    blank(st, 0)
                    if st.index == 0:
                        blank(st, 1)

            def norm_rstd(t):
                pool.wait_ge(ln_sums, t.G + 1)
                g.tensor_tensor(veps[:, :], mv[:, :, 1], epsb[:, t.st.index // 3, :], ALU.add)\
                    .then_inc(ln_veps, 1)
                pool.wait_ge(ln_veps, t.G + 1)
                g.tensor_tensor(rstd[:, :], veps[:, :], halfpow[:, :], ALU.pow).then_inc(ln_rstd, 1)
                pool.wait_ge(x_in[t.par], 32 * (t.GP + 1))
                g.tensor_tensor(xb[t.par][:, :, :], xt[t.par][:, :, :],
                                rowsb[:, t.st.index, :].unsqueeze(1).to_broadcast([P, TT, D]), ALU.add)\
                    .then_inc(xb_ready, 1)

            def ctx_norm_rstd(t):
                st = t.st
                pool.wait_ge(st.ctx_sums, t.B + 1)
                g.tensor_tensor(cveps[0:NC, :], cmv[0:NC, 1:2], epsb[0:NC, 0, 0:1], ALU.add)\
                    .then_inc(st.ctx_veps, 1)
                pool.wait_ge(st.ctx_veps, t.B + 1)
                g.tensor_tensor(crstd[0:NC, :], cveps[0:NC, :], halfpow[0:NC, 0:1], ALU.pow)\
                    .then_inc(st.ctx_rstd, 1)

            def finish_qk(t, j):
                st, B = t.st, t.B
                kv = kview(t)
                if st.rope:
                    half = st.NQK // 2
                    isk = j >= half
                    cols_ = st.NK if isk else N
                    m = 2 * (j % half)
                    view = lambda buf: buf[:, 0:2 * cols_].rearrange("p (m n) -> p m n", m=2)
                    pool.wait_ge(st.qk_raw, B * st.NQK + j + 1)
                    sin = ropesb[:, 3 if isk else 1, 0:cols_].unsqueeze(1).to_broadcast([P, 2, cols_])
                    g.tensor_tensor(view(sh[j % 2]), view(sh[j % 2]), sin, ALU.mult).then_inc(st.rope_step, 1)
                    pool.wait_ge(st.rope_step, B * st.NQK + j + 1)
                    if not isk:
                        g.tensor_tensor(qT[t.par][:, m:m + 2, :], view(t1[j % 2]), view(sh[j % 2]), ALU.add)\
                            .then_inc(st.qk_out, 1)
                    else:
                        for hh in (0, 1):
                            r = slice(64 * hh, 64 * hh + 64)
                            dst = kv[r, 2 * m + hh:2 * m + 4:2, :]
                            last = g.tensor_tensor(dst, view(t1[j % 2])[r], view(sh[j % 2])[r], ALU.add)
                        last.then_inc(st.qk_out, 1)
                        pool.wait_ge(st.qk_out, B * st.NQK + j + 1)
                elif j == 1:
                    pool.wait_ge(st.qk_raw, B * 2 + 2)
                    for m in (0, 1):
                        last = g.tensor_tensor(
                            kv[:, 8 * m:8 * m + 8, :],
                            ksb[:, m, 0:st.NK].unsqueeze(1).to_broadcast([P, 8, st.NK]),
                            headmask[:, :].unsqueeze(2).to_broadcast([P, 8, st.NK]), ALU.mult)
                    last.then_inc(st.qk_out, 1)

            def run(own, nxt, jobs, steps):
                for whose, what, j in steps:
                    if what == "LN":
                        norm_rstd(nxt)
                    elif what == "CN" and nxt.st.rope:
                        ctx_norm_rstd(nxt)
                    elif what == "QK":
                        finish_qk(nxt, j)
                    elif what == "F1":
                        pool.wait_ge(own.st.g_f32, own.B * 4 + j + 1)
                        g.tensor_tensor(oT[:, HI, 2 * j:2 * j + 2, :].rearrange("p m n -> p (m n)"),
                                        t1[j % 2][:, :], zero[:, :].to_broadcast([P, 2 * N]), ALU.add)\
                            .then_inc(own.st.g_hi, 1)

            def begin(st):
                if st.att and st.index:
                    pool.wait_ge(y_ready, NB * st.index)
                    blank(st, 1)

            walk(pool, run, enter, begin)

        @block.scalar
        def _(act):
            a = nc.scalar
            def load_chunk(st, c):
                for col_, rows_, n, src in chunks[st.index][c]:
                    act.dma_start(wload[chunks_before(st, c) % 2][0:rows_, col_:col_ + n], src)\
                        .then_inc(w_in[chunks_before(st, c) % 2], 16)

            def begin(st):
                if st.index + 1 < len(stages):
                    nxt = stages[st.index + 1]
                    act.wait_ge(w_ready, chunks_before(nxt, 0))
                    for c in range(2):
                        load_chunk(nxt, c)

            act.wait_ge(blank0, 1)
            for c in range(2):
                load_chunk(stages[0], c)
            act.wait_ge(param_in, 64)
            a.activation(esb[:, :, :], condsb[:, :, :], ACT.Exp, scale=-1.0).then_inc(silu_step, 1)
            a.activation(bq4[:, :], colsb[:, COLS["b_qk"]:COLS["b_qk"] + 2], ACT.Copy, scale=0.25)\
                .then_inc(silu_step, 1)
            act.wait_ge(silu_step, 2)

            def col(name, c, rows_=P):
                return colsb[0:rows_, COLS[name] + c:COLS[name] + c + 1]

            def run(own, nxt, jobs, steps):
                    for whose, what, j in steps:
                        t = own if whose == "own" else nxt
                        st, B = t.st, t.B
                        if what in JOBS:
                            k, before, count = jobs.slot()
                            ps = ps_j[k]
                            pv = ps[:, :].rearrange("p (m n) -> p m n", m=2)
                        if what == "W":
                            ws, c = j
                            at = chunks_before(ws, c)
                            if 1 <= c < ws.chunks - 1:
                                act.wait_ge(w_ready, at)
                                load_chunk(ws, c + 1)
                            act.wait_ge(w_in[at % 2], 16 * (loads_before(ws, c) + len(chunks[ws.index][c])))
                            a.activation(wsplit[ws.index % 2][:, HI, c * CHUNK:(c + 1) * CHUNK],
                                         wload[at % 2][:, :], ACT.Copy, scale=W_SCALE).then_inc(w_hi, 1)
                        elif what == "LNT":
                            act.wait_ge(pj_ready, count)
                            act.wait_ge(x_in[t.par], 32 * (t.GP + 1))
                            c = coef[t.par]
                            a.activation(h32[:, 0, :], pv[:, 0, :], ACT.Identity, scale=c[:, 0:1], bias=c[:, 2:3])
                            a.activation(h32[:, 1, :], pv[:, 1, :], ACT.Identity, scale=c[:, 1:2], bias=c[:, 3:4])\
                                .then_inc(h_f32, 1)
                            act.wait_ge(h_f32, t.G + 1)
                            act.sem_inc(pj_free[k], 1)
                            a.activation(hT[:, HI], h32[:, :, :], ACT.Copy).then_inc(h_hi, 1)
                        elif what in ("CT", "CP"):
                            act.wait_ge(pj_ready, count)
                            per = 1 if st.rope else 2
                            nth = B * per + (what == "CP") + 1
                            rows_ = P if what == "CP" else DC - P
                            for m, r in ((0, P), (1, rows_)):
                                src = ps[0:r, m * NC:(m + 1) * NC]
                                if what == "CP":
                                    last = a.activation(c32[0:r, m, :], src, ACT.Identity, scale=1 / W_SCALE,
                                                        bias=col("b_ctx", m))
                                elif st.rope:
                                    last = a.activation(c32[0:r, m, :], src, ACT.Identity,
                                                        scale=col("lnc_w", m, r), bias=col("lnc_b", m, r))
                                else:
                                    last = a.activation(c32[0:r, m, :], src, ACT.Copy)
                            last.then_inc(st.c_f32, 1)
                            act.wait_ge(st.c_f32, nth)
                            act.sem_inc(pj_free[k], 1)
                            dst = cT if what == "CP" or st.rope else cRaw
                            a.activation(dst[:, HI, 0, :], c32[:, 0, :], ACT.Copy)
                            a.activation(dst[0:rows_, HI, 1, :], c32[0:rows_, 1, :], ACT.Copy).then_inc(st.c_hi, 1)
                        elif what == "QK" and not st.rope:
                            act.wait_ge(pj_ready, count)
                            for m in (0, 1):
                                if j == 0:
                                    last = a.activation(qT[t.par][:, m, :], pv[:, m, :], ACT.Identity, scale=0.25 / W_SCALE,
                                                        bias=0.0 if st.cross else bq4[:, m:m + 1])
                                else:
                                    if m == 0 and not (isinstance(B, int) and B == 0):
                                        act.wait_ge(st.qk_out, B)
                                    last = a.activation(ksb[:, m, 0:st.NK], ps[:, m * st.NK:(m + 1) * st.NK],
                                                        ACT.Identity, scale=1 / W_SCALE,
                                                        bias=0.0 if st.cross else col("b_qk", 2 + m))
                            last.then_inc(st.qk_raw, 1)
                            act.wait_ge(st.qk_raw, B * 2 + j + 1)
                            act.sem_inc(pj_free[k], 1)
                        elif what == "V":
                            if st.vbias:
                                act.wait_ge(st.v_raw, B + 1)
                                for tt in range(TT):
                                    last = a.activation(vview(t)[:, HI, tt, :, 0:16],
                                                        v32[:, tt, :].rearrange("p (h d) -> p h d", h=H), ACT.Copy)
                            else:
                                act.wait_ge(pj_ready, count)
                                tt, h0, nh = (j // 2, 8 * (j % 2), 8) if st.DH == 64 else (0, 0, H)
                                last = a.activation(vview(t)[0:st.KP, HI, tt, h0:h0 + nh, 0:st.DH],
                                                    ps[0:st.KP, 0:nh * st.DH].rearrange("p (h d) -> p h d", h=nh),
                                                    ACT.Copy, scale=1 / W_SCALE)
                            last.then_inc(st.v_hi, 1)
                        elif what == "E":
                            act.wait_ge(st.max_ready, B * st.U + j + 1)
                            if j >= 2:
                                act.wait_ge(st.pt_ready, B * st.U + j - 1)
                            for hh in range(st.HU):
                                c = slice(hh * st.NK, (hh + 1) * st.NK)
                                last = a.activation(prob[j % 2][:, c], ps_s[j % 2][:, c], ACT.Exp,
                                                    bias=negmax[j % 2][:, hh:hh + 1])
                            last.then_inc(st.p_ready, 1)
                        elif what == "T":
                            act.wait_ge(st.pt_ready, B * st.U + j + 1)
                            if j >= 4:
                                act.wait_ge(st.av_done, B * st.U + j - 3)
                            a.activation(probT[j % 4][0:st.KP, HI, :], ps_t[j % 2][0:st.KP, :], ACT.Copy,
                                         scale=P_SCALE).then_inc(st.pt_hi, 1)
                        elif what == "OT":
                            act.wait_ge(pj_ready, count)
                            g_, tt = j // TT, j % TT
                            a.activation(oT[:, HI, 2 * g_:2 * g_ + 2, tt * P:tt * P + P],
                                         ps[:, 0:256].rearrange("p (f n) -> p f n", f=2), ACT.Copy)\
                                .then_inc(st.oT_hi, 1)
                        elif what == "F1":
                            act.wait_ge(pj_ready, count)
                            if j >= 2:
                                act.wait_ge(st.g_ready, B * 4 + j - 1)
                            name = "ff_b1" if st.index == 2 else "b_fc1"
                            for m in (0, 1):
                                last = a.activation(t1[j % 2][:, m * N:(m + 1) * N], pv[:, m, :], st.gelu,
                                                    scale=1 / W_SCALE, bias=col(name, 2 * j + m))
                            last.then_inc(st.g_f32, 1)
                            act.wait_ge(st.g_f32, B * 4 + j + 1)
                            act.sem_inc(pj_free[k], 1)

            walk(act, run, lambda st: None, begin)

        @block.vector
        def _(dve):
            v = nc.vector
            dve.wait_ge(silu_step, 2)
            v.tensor_scalar(esb[:, :, :], esb[:, :, :], 1.0, None, ALU.add).then_inc(mod_step, 1)
            dve.wait_ge(mod_step, 1)
            v.reciprocal(esb[:, :, :], esb[:, :, :]).then_inc(mod_step, 1)
            dve.wait_ge(mod_step, 2)
            v.tensor_tensor(silub[:, :, :], esb[:, :, :], condsb[:, :, :], ALU.mult).then_inc(mod_step, 1)
            dve.wait_ge(mod_mm, 1)
            bias_at = [COLS["g1_b"] + c for c in range(8)] + [COLS["b_ada"] + c for c in range(12)]
            gains = (0, 1, 4, 5, 10, 11, 14, 15, 18, 19)
            for c, at in enumerate(bias_at):
                last = v.tensor_scalar(modsb[:, c, :], ps_j[0][:, c * NB:(c + 1) * NB], colsb[:, at:at + 1],
                                       1.0 if c in gains else 0.0, ALU.add, ALU.add)
            last.then_inc(mod_step, 1)
            dve.wait_ge(mod_step, 4)
            for s in range(5):
                for k in range(KD):
                    if s < 2:
                        w = colsb[:, COLS[("ln1_w", "ln2_w")[s]] + k:COLS[("ln1_w", "ln2_w")[s]] + k + 1]
                        b_ = colsb[:, COLS[("ln1_b", "ln2_b")[s]] + k:COLS[("ln1_b", "ln2_b")[s]] + k + 1]
                        gain, shift = modsb[:, 4 * s + k, :], modsb[:, 4 * s + 2 + k, :]
                        v.tensor_scalar(coefsb[:, s, :, k], gain, w, None, ALU.mult)
                        last = v.scalar_tensor_tensor(coefsb[:, s, :, 2 + k], gain, b_, shift, ALU.mult, ALU.add)
                    else:
                        c = 8 + 4 * (s - 2)
                        v.tensor_copy(coefsb[:, s, :, k], modsb[:, c + 2 + k, :])
                        last = v.tensor_copy(coefsb[:, s, :, 2 + k], modsb[:, c + k, :])
            last.then_inc(coef_ready, 1)
            dve.wait_ge(param_in, 64)
            dve.wait_ge(ident_step, 6)

            def norm(t):
                xs_ = xt[t.par]
                dve.wait_ge(x_in[t.par], 32 * (t.GP + 1))
                for tt in range(TT):
                    last = v.bn_stats(stats[:, tt, :], xs_[:, tt, :])
                last.then_inc(ln_stats, 1)
                dve.wait_ge(ln_stats, t.G + 1)
                v.memset(tick[:, :], 0.0)
                for tt in range(TT):
                    last = v.bn_aggr(mv[:, tt, :], stats[:, tt, :])
                last.then_inc(ln_sums, 1)
                dve.wait_ge(ln_rstd, t.G + 1)
                if not (isinstance(t.G, int) and t.G == 0):
                    dve.wait_ge(h_ready, t.G)
                for tt in range(TT):
                    last = v.tensor_scalar(xhat[:, tt, :], xs_[:, tt, :], mv[:, tt, 0:1],
                                           rstd[:, tt:tt + 1], ALU.subtract, ALU.mult)
                last.then_inc(xhat_ready, 1)

            def norm_ctx(t):
                st = t.st
                rows_ = ctxt[t.par][0:NC, :]
                dve.wait_ge(st.ctx_in[t.par], 16 * (t.i + 1))
                if not (isinstance(t.B, int) and t.B == 0):
                    dve.wait_ge(st.cT_ready, t.B)
                if st.rope:
                    v.bn_stats(cstats[0:NC, :], rows_).then_inc(st.ctx_stats, 1)
                    dve.wait_ge(st.ctx_stats, t.B + 1)
                    v.memset(tick[:, :], 0.0)
                    v.bn_aggr(cmv[0:NC, :], cstats[0:NC, :]).then_inc(st.ctx_sums, 1)
                    dve.wait_ge(st.ctx_rstd, t.B + 1)
                    v.tensor_scalar(chat[0:NC, :], rows_, cmv[0:NC, 0:1], crstd[0:NC, 0:1],
                                    ALU.subtract, ALU.mult).then_inc(st.chat_ready, 1)
                else:
                    v.tensor_copy(chat[0:NC, :], rows_).then_inc(st.chat_ready, 1)

            def run(own, nxt, jobs, steps):
                    for whose, what, j in steps:
                        t = own if whose == "own" else nxt
                        st, B = t.st, t.B
                        if what in JOBS:
                            k, before, count = jobs.slot()
                            ps = ps_j[k]
                        if what == "W":
                            ws, c = j
                            at = chunks_before(ws, c)
                            dve.wait_ge(w_hi, at + 1)
                            dst = wsplit[ws.index % 2][:, :, c * CHUNK:(c + 1) * CHUNK]
                            v.scalar_tensor_tensor(dst[:, LO], wload[at % 2][:, :], W_SCALE, dst[:, HI],
                                                   ALU.mult, ALU.subtract).then_inc(w_ready, 1)
                        elif what == "LNT":
                            dve.wait_ge(h_hi, t.G + 1)
                            v.tensor_tensor(hT[:, LO], h32[:, :, :], hT[:, HI], ALU.subtract)\
                                .then_inc(h_ready, 1)
                        elif what in ("CT", "CP"):
                            per = 1 if st.rope else 2
                            dve.wait_ge(st.c_hi, B * per + (what == "CP") + 1)
                            dst, done = (cT, st.cT_ready) if what == "CP" or st.rope else (cRaw, st.c_raw)
                            rows_ = P if what == "CP" else DC - P
                            v.tensor_tensor(dst[:, LO, 0, :], c32[:, 0, :], dst[:, HI, 0, :], ALU.subtract)
                            v.tensor_tensor(dst[0:rows_, LO, 1, :], c32[0:rows_, 1, :], dst[0:rows_, HI, 1, :],
                                            ALU.subtract).then_inc(done, 1)
                        elif what == "OT":
                            dve.wait_ge(st.oT_hi, B * st.NO + j + 1)
                            g_, tt = j // TT, j % TT
                            dst = oT[:, :, 2 * g_:2 * g_ + 2, tt * P:tt * P + P]
                            v.tensor_tensor(dst[:, LO], ps[:, 0:256].rearrange("p (f n) -> p f n", f=2),
                                            dst[:, HI], ALU.subtract).then_inc(st.oT_done, 1)
                            dve.wait_ge(st.oT_done, B * st.NO + j + 1)
                            dve.sem_inc(pj_free[k], 1)
                        elif what == "F1":
                            dve.wait_ge(st.g_hi, B * 4 + j + 1)
                            dst = oT[:, :, 2 * j:2 * j + 2, :]
                            v.tensor_tensor(dst[:, LO], t1[j % 2][:, :].rearrange("p (m n) -> p m n", m=2),
                                            dst[:, HI], ALU.subtract).then_inc(st.g_ready, 1)
                        elif what == "LN":
                            norm(t)
                        elif what == "CN":
                            norm_ctx(t)
                        elif what == "QK" and st.rope:
                            half = st.NQK // 2
                            isk = j >= half
                            n = st.NK if isk else N
                            dve.wait_ge(pj_ready, count)
                            if j >= 2:
                                dve.wait_ge(st.qk_out, B * st.NQK + j - 1)
                            cos = ropesb[:, 2 if isk else 0, 0:n].unsqueeze(1).to_broadcast([P, 2, n])
                            v.tensor_tensor(t1[j % 2][:, 0:2 * n].rearrange("p (m n) -> p m n", m=2),
                                            ps[:, 0:2 * n].rearrange("p (m n) -> p m n", m=2), cos, ALU.mult)
                            v.stream_shuffle(sh[j % 2][:, 0:2 * n], ps[:, 0:2 * n], [c ^ 1 for c in range(32)])\
                                .then_inc(st.qk_raw, 1)
                            dve.wait_ge(st.qk_raw, B * st.NQK + j + 1)
                            dve.sem_inc(pj_free[k], 1)
                        elif what == "V":
                            if st.vbias:
                                dve.wait_ge(pj_ready, count)
                                for tt in range(TT):
                                    last = v.scalar_tensor_tensor(v32[:, tt, :], ps[:, tt * D:(tt + 1) * D],
                                                                  1 / W_SCALE, rowsb[:, 6, :], ALU.mult, ALU.add)
                                last.then_inc(st.v_raw, 1)
                                dve.wait_ge(st.v_hi, B + 1)
                                for tt in range(TT):
                                    dst = vview(t)[:, :, tt, :, 0:16]
                                    last = v.tensor_tensor(dst[:, LO], v32[:, tt, :].rearrange("p (h d) -> p h d", h=H),
                                                           dst[:, HI], ALU.subtract)
                            else:
                                dve.wait_ge(st.v_hi, B * st.NV + j + 1)
                                tt, h0, nh = (j // 2, 8 * (j % 2), 8) if st.DH == 64 else (0, 0, H)
                                dst = vview(t)[0:st.KP, :, tt, h0:h0 + nh, 0:st.DH]
                                last = v.scalar_tensor_tensor(
                                    dst[:, LO], ps[0:st.KP, 0:nh * st.DH].rearrange("p (h d) -> p h d", h=nh),
                                    1 / W_SCALE, dst[:, HI], ALU.mult, ALU.subtract)
                            last.then_inc(st.v_ready, 1)
                            dve.wait_ge(st.v_ready, B * st.NV + j + 1)
                            dve.sem_inc(pj_free[k], 1)
                        elif what == "S":
                            dve.wait_ge(st.s_ready, B * st.U + j + 1)
                            if j >= 2:
                                dve.wait_ge(st.p_ready, B * st.U + j - 1)
                            v.tensor_reduce(negmax[j % 2][:, 0:st.HU],
                                            ps_s[j % 2][:, 0:st.HU * st.NK].rearrange("p (h n) -> p h n", h=st.HU),
                                            AX_X, ALU.max, negate=True).then_inc(st.max_ready, 1)
                        elif what == "T":
                            dve.wait_ge(st.pt_hi, B * st.U + j + 1)
                            dst = probT[j % 4][0:st.KP]
                            v.scalar_tensor_tensor(dst[:, LO], ps_t[j % 2][0:st.KP, :], P_SCALE, dst[:, HI],
                                                   ALU.mult, ALU.subtract).then_inc(st.pt_copied, 1)
                        elif what == "AV" and j % st.UI == st.UI - 1:
                            n = j // st.UI
                            dve.wait_ge(st.av_done, B * st.U + j + 1)
                            w = st.DH + 1
                            o = ps_o[n % 2][:, 0:st.HG * w].rearrange("p (h d) -> p h d", h=st.HG)
                            v.reciprocal(rinv[n % 2][:, 0:st.HG], o[:, :, st.DH]).then_inc(st.rinv_ready, 1)
                            dve.wait_ge(st.rinv_ready, B * st.NO + n + 1)
                            if n >= 2:
                                dve.wait_ge(st.oT_done, B * st.NO + n - 1)
                            v.tensor_tensor(osb[n % 2][:, :].rearrange("p (h d) -> p h d", h=st.HG),
                                            o[:, :, 0:st.DH],
                                            rinv[n % 2][:, 0:st.HG].unsqueeze(2).to_broadcast([P, st.HG, st.DH]),
                                            ALU.mult).then_inc(st.o_ready, 1)
                        elif what == "WO":
                            dve.wait_ge(pj_ready, count)
                            dve.wait_ge(xb_ready, t.G + 1)
                            if True:
                                dve.wait_ge(stored[t.par], 16 * t.GP + 1)
                            v.scalar_tensor_tensor(yt[t.par][:, :, :], ps[:, :].rearrange("p (t d) -> p t d", t=TT),
                                                   1 / W_SCALE, xb[t.par][:, :, :], ALU.mult, ALU.add)\
                                .then_inc(y_ready, 1)
                            dve.wait_ge(y_ready, t.G + 1)
                            dve.sem_inc(pj_free[k], 1)

            walk(dve, run, lambda st: None)

        @block.tensor
        def _(pe):
            te = nc.tensor
            pe.wait_ge(param_in, 64)
            pe.wait_ge(mod_w_in, 16 * len(weights["mod"]))
            pe.wait_ge(mod_step, 3)
            tile = 0
            for name, k_, n_, at, _src in weights["mod"]:
                w = mod_w[name][:, at:at + k_ * n_].rearrange("p (k n) -> p k n", k=k_)
                src = silub if name == "W_ada" else condsb
                for m in range(n_ // P):
                    for k in range(KD):
                        last = te.matmul(ps_j[0][:, tile * NB:(tile + 1) * NB], w[:, k, m * P:(m + 1) * P],
                                         src[:, k, :], start=(k == 0), stop=(k == KD - 1))
                    tile += 1
            last.then_inc(mod_mm, 1)
            pe.wait_ge(coef_ready, 1)
            pe.wait_ge(ident_step, 6)
            for k in (0, 1):
                pe.sem_inc(pj_free[k], 1)

            def enter(st):
                if st.index:
                    pe.wait_ge(w_ready, chunks_before(st, st.chunks))

            def project(ps_out, lhsT, rhs, rows_):
                todo = [(k, r, a_, b_) for k, r in enumerate(rows_) for a_, b_ in PARTS]
                for n, (k, r, a_, b_) in enumerate(todo):
                    last = te.matmul(ps_out, lhsT(a_, k, r), rhs(b_, k, r), start=(n == 0),
                                     stop=(n == len(todo) - 1))
                return last

            def run(own, nxt, jobs, steps):
                    for whose, what, j in steps:
                        t = own if whose == "own" else nxt
                        st, B = t.st, t.B
                        if what in JOBS:
                            k_, before, _count = jobs.slot()
                            ps = ps_j[k_]
                            pv = ps[:, :].rearrange("p (m n) -> p m n", m=2)
                            pe.wait_ge(pj_free[k_], before + 1)
                        if what == "LNT" and st.index == 0 and own is None:
                            pe.wait_ge(w_ready, chunks_before(st, st.chunks))
                        if what == "LNT":
                            pe.wait_ge(xhat_ready, t.G + 1)
                            for f in range(KD):
                                for tt in range(TT):
                                    last = te.transpose(pv[:, f, tt * P:(tt + 1) * P],
                                                        xhat[:, tt, f * P:(f + 1) * P], ident[:, :])
                        elif what == "CT":
                            pe.wait_ge(st.chat_ready, B + 1)
                            te.transpose(ps[:, 0:NC], chat[0:NC, 0:P], ident[0:NC, 0:NC])
                            last = te.transpose(ps[0:64, NC:2 * NC], chat[0:NC, P:DC], ident[0:NC, 0:NC])
                        elif what == "CP":
                            pe.wait_ge(st.c_raw, B + 1)
                            w = wview(st, "wctx")
                            for m in (0, 1):
                                last = project(ps[:, m * NC:(m + 1) * NC],
                                               lambda s, k, r: w[0:r, s, k, m * P:(m + 1) * P],
                                               lambda s, k, r: cRaw[0:r, s, k, :], (P, DC - P))
                        elif what == "QK":
                            half = st.NQK // 2
                            isk = j >= half
                            if j == 0:
                                pe.wait_ge(h_ready, t.G + 1)
                            if j == half and st.cross:
                                pe.wait_ge(st.cT_ready, B + 1)
                            w = wview(st, "wk" if isk else "wq")
                            n = st.NK if isk else N
                            src = cT if isk and st.cross else hT
                            rows_ = (P, DC - P) if isk and st.cross and st.rope else (P, P)
                            for mm in (0, 1):
                                m = 2 * (j % half) + mm
                                last = project(ps[:, mm * n:(mm + 1) * n],
                                               lambda s, k, r: w[0:r, s, k, m * P:(m + 1) * P],
                                               lambda s, k, r: src[0:r, s, k, 0:n], rows_)
                        elif what == "V":
                            w = wview(st, "wv")
                            src = cT if st.cross else hT
                            rows_ = (P, DC - P) if st.cross and st.rope else (P, P)
                            if st.DH == 64:
                                tt, hf = j // 2, j % 2
                                last = project(ps[0:st.KP, :],
                                               lambda s, k, r: src[0:r, s, k, tt * P:tt * P + st.KP],
                                               lambda s, k, r: w[0:r, s, k, hf * 512:(hf + 1) * 512], rows_)
                            else:
                                for tt in range(st.KT):
                                    last = project(ps[0:st.KP, tt * 256:(tt + 1) * 256],
                                                   lambda s, k, r: src[0:r, s, k, tt * P:tt * P + st.KP],
                                                   lambda s, k, r: w[0:r, s, k, :], rows_)
                        elif what == "S":
                            if j == 0:
                                if st.rope:
                                    pe.wait_ge(st.qk_out, (B + 1) * st.NQK)
                                else:
                                    pe.wait_ge(st.qk_raw, (B + 1) * 2)
                                    pe.wait_ge(st.qk_out, B + 1)
                            if j >= 2:
                                pe.wait_ge(st.p_ready, B * st.U + j - 1)
                            grp, rest = j // (TT * st.UI), j % (TT * st.UI)
                            tt, h0 = rest // st.UI, grp * st.HG + (rest % st.UI) * st.HU
                            kv = kview(t)
                            step = min(st.HU, st.TH)
                            for h in range(h0, h0 + st.HU, step):
                                c = (h - h0) * st.NK
                                last = te.matmul(ps_s[j % 2][:, c:c + step * st.NK],
                                                 qT[t.par][:, h // st.TH, tt * P:(tt + 1) * P],
                                                 kv[:, h:h + step, :], start=True, stop=True)
                            last.then_inc(st.s_ready, 1)
                        elif what == "T":
                            pe.wait_ge(st.p_ready, B * st.U + j + 1)
                            if j >= 2:
                                pe.wait_ge(st.pt_copied, B * st.U + j - 1)
                            for blk in range(4):
                                last = te.transpose(ps_t[j % 2][0:st.KP, blk * P:(blk + 1) * P],
                                                    prob[j % 2][:, blk * st.KP:(blk + 1) * st.KP], ident[:, :])
                            last.then_inc(st.pt_ready, 1)
                        elif what == "AV":
                            if j == 0:
                                pe.wait_ge(st.v_ready, (B + 1) * st.NV)
                                pe.wait_ge(kv_blank, 2 * st.order + t.par + 1)
                            pe.wait_ge(st.pt_copied, B * st.U + j + 1)
                            n = j // st.UI
                            if j % st.UI == 0:
                                if n >= 2:
                                    pe.wait_ge(st.o_ready, B * st.NO + n - 1)
                            grp, rest = j // (TT * st.UI), j % (TT * st.UI)
                            w = st.DH + 1
                            for hh in range(st.HU):
                                pos = (rest % st.UI) * st.HU + hh
                                for kt in range(st.KT):
                                    blk = hh * st.KT + kt
                                    for n_part, (pp, vp) in enumerate(PARTS):
                                        last = te.matmul(ps_o[n % 2][:, pos * w:(pos + 1) * w],
                                                         probT[j % 4][0:st.KP, pp, blk * P:(blk + 1) * P],
                                                         vview(t)[0:st.KP, vp, kt, grp * st.HG + pos, :],
                                                         start=(kt == 0 and n_part == 0),
                                                         stop=(kt == st.KT - 1 and n_part == 2))
                            last.then_inc(st.av_done, 1)
                        elif what == "OT":
                            pe.wait_ge(st.o_ready, B * st.NO + j + 1)
                            for f in (0, 1):
                                last = te.transpose(ps[:, f * P:(f + 1) * P], osb[j % 2][:, f * P:(f + 1) * P],
                                                    ident[:, :])
                        elif what == "F1":
                            if j == 0:
                                pe.wait_ge(h_ready, t.G + 1)
                            w = wview(st, "w1")
                            for mm in (0, 1):
                                m = 2 * j + mm
                                last = project(pv[:, mm, :], lambda s, k, r: w[:, s, k, m * P:(m + 1) * P],
                                               lambda s, k, r: hT[:, s, k, :], (P, P))
                        elif what == "WO":
                            w = wview(st, "wo")
                            if st.att:
                                pe.wait_ge(st.oT_done, (B + 1) * st.NO)
                                kt_n = st.M
                            else:
                                pe.wait_ge(st.g_ready, (B + 1) * 4)
                                kt_n = 8
                            for tt in range(TT):
                                last = project(pv[:, tt, :], lambda s, k, r: oT[:, s, k, tt * P:(tt + 1) * P],
                                               lambda s, k, r: w[:, s, k, :], (P,) * kt_n)
                        if what in JOBS:
                            last.then_inc(pj_ready, 1)

            walk(pe, run, enter)


def kernel(**inputs):
    import concourse.bacc as _bacc
    from concourse import mybir as _mybir
    from concourse.bass_utils import run_bass_kernel_spmd as _run

    nc = _bacc.Bacc("TRN2", target_bir_lowering=False, num_devices=1)
    arrays = {}

    def dram(name, a):
        a = np.ascontiguousarray(a)
        arrays[name] = a
        return nc.dram_tensor(name, a.shape, _mybir.dt.from_np(a.dtype), kind="ExternalInput").ap()

    L0, L1 = "L0_xcond_", "L1_xcond_"
    g = {k: np.asarray(v) for k, v in inputs.items()}

    def columns(v):
        v = np.concatenate([v, np.zeros((-len(v)) % P, v.dtype)])
        return v.reshape(-1, P).T

    qkv_b = g[L1 + "b_qkv"]
    order = [g[L0 + "ln1_w"], g[L0 + "ln1_b"], g[L0 + "ln2_w"], g[L0 + "ln2_b"], g[L0 + "g1_b"], g[L0 + "b1_b"],
             g[L0 + "g2_b"], g[L0 + "b2_b"], g[L0 + "ca_lnc_w"], g[L0 + "ca_lnc_b"], g[L0 + "ff_b1"],
             g[L1 + "b_ada"], qkv_b[0:2 * D], g[L1 + "b_ctx"], g[L1 + "b_fc1"]]
    cols = dram("in_cols", np.concatenate([columns(v) for v in order], axis=1))
    condT = dram("in_condT", g["cond_1024"].reshape(NB, KD, P).transpose(2, 1, 0))
    rows = dram("in_rows", np.stack([g[L0 + "sa_bo"], g[L0 + "ca_bo"], g[L0 + "ff_b2"], g[L1 + "b_proj"],
                                     g[L1 + "b_out"], g[L1 + "b_fc2"], qkv_b[2 * D:3 * D]]))

    f32 = np.float32
    inv = (f32(1.0) / np.power(f32(10000.0), np.arange(0, 64, 2, dtype=f32) / f32(64))).astype(f32)
    ang = (np.arange(N, dtype=f32)[:, None] * inv[None, :]).astype(f32)
    sin, cos = np.sin(ang.astype(np.float64)), np.cos(ang.astype(np.float64))
    freq = (np.arange(P) % 64) // 2
    sign = np.where(np.arange(P) % 2 == 0, -1.0, 1.0)[:, None]
    c, s = cos.T[freq], sin.T[freq] * sign
    ropes = dram("in_ropes", (np.stack([c * 0.125, s * 0.125, c, s], axis=1) / W_SCALE).astype(f32))

    def w(name):
        return dram("in_" + name, g[name])

    def place(*items):
        out, at = {}, 0
        for name, src, n in items:
            k = -(-src.shape[0] // P)
            out[name] = (src, k, n, at)
            at += k * n
        return out

    sakv, cakv, qkv = w(L0 + "sa_wkv"), w(L0 + "ca_wkv"), w(L1 + "W_qkv")
    weights = {
        0: place(("wq", w(L0 + "sa_wq"), 1024), ("wk", sakv[:, 0:1024], 1024), ("wv", sakv[:, 1024:2048], 1024),
                 ("wo", w(L0 + "sa_wo"), 256)),
        1: place(("wq", w(L0 + "ca_wq"), 1024), ("wk", cakv[:, 0:1024], 1024), ("wv", cakv[:, 1024:2048], 1024),
                 ("wo", w(L0 + "ca_wo"), 256)),
        2: place(("w1", w(L0 + "ff_w1"), 1024), ("wo", w(L0 + "ff_w2"), 256)),
        3: place(("wq", qkv[:, 0:256], 256), ("wk", qkv[:, 256:512], 256), ("wv", qkv[:, 512:768], 256),
                 ("wo", w(L1 + "W_proj"), 256)),
        4: place(("wctx", w(L1 + "W_ctx"), 256), ("wq", w(L1 + "W_q"), 256), ("wk", w(L1 + "W_k"), 256),
                 ("wv", w(L1 + "W_v"), 256), ("wo", w(L1 + "W_out"), 256)),
        5: place(("w1", w(L1 + "W_fc1"), 1024), ("wo", w(L1 + "W_fc2"), 256)),
    }
    mod, at = [], 0
    for name in ("g1_w", "b1_w", "g2_w", "b2_w", "W_ada"):
        src = w((L1 if name == "W_ada" else L0) + name)
        mod.append((name, KD, src.shape[1], at if name != "W_ada" else 0, src))
        at += KD * src.shape[1]
    weights["mod"] = mod
    x = dram("in_x", g["x"])
    context = dram("in_ctx", g["ctx_768"])
    out = nc.dram_tensor("out_0", [NB, N, D], _mybir.dt.float32, kind="ExternalOutput").ap()
    build(nc, x, context, condT, cols, ropes, rows, weights, out)
    r = _run(nc, [arrays], core_ids=[0])
    return r.results[0]["out_0"]
```

```python
from contextlib import ExitStack

import numpy as np

import concourse.bass as bass
from concourse import mybir

F32 = mybir.dt.float32
F16 = mybir.dt.float16
ALU = mybir.AluOpType
ACT = mybir.ActivationFunctionType
AX_X = mybir.AxisListType.X

P = 128
NB, N, D = 8, 256, 256
KD = D // P
TT = N // P
H = 16
NC, DC = 120, 192
TURNS = NB // 2

HI, LO = 0, 1
PARTS = ((HI, HI), (HI, LO), (LO, HI))
W_SCALE = 64.0
P_SCALE = 1024.0
EARLY_CHUNKS = 4
CHUNK = 1024

COLS = {}


def _columns():
    at = 0
    for name, c in (("ln1_w", 2), ("ln1_b", 2), ("ln2_w", 2), ("ln2_b", 2), ("g1_b", 2), ("b1_b", 2),
                    ("g2_b", 2), ("b2_b", 2), ("lnc_w", 2), ("lnc_b", 2), ("ff_b1", 8), ("b_ada", 12),
                    ("b_qk", 4), ("b_ctx", 2), ("b_fc1", 8)):
        COLS[name] = at
        at += c
    return at


NCOLS = _columns()


class Stage:

    def __init__(self, nc, ctx, index, name, kind, coef, eps, DH=0, cross=False, rope=False, gelu=None, order=0):
        self.index, self.name, self.kind, self.coef, self.eps = index, name, kind, coef, eps
        self.cross, self.rope, self.gelu, self.order = cross, rope, gelu, order
        self.att = kind == "att"

        def sem(what):
            return ctx.enter_context(nc.semaphore(f"{name}_{what}"))

        if self.att:
            self.DH = DH
            self.NK = NC if cross else N
            self.KP = NC if cross else P
            self.KT = self.NK // self.KP
            self.TH = P // DH
            self.M = H * DH // P
            self.HU = 4 if cross else 2
            self.HG = 256 // DH
            self.NG = H // self.HG
            self.UI = self.HG // self.HU
            self.U = self.NG * TT * self.UI
            self.NO = self.NG * TT
            self.ahead = 4 if cross else 6
            self.NQK = self.M
            self.NV = (2 * self.KT) if DH == 64 else 1
            self.s_ready = sem("s_ready")
            self.max_ready = sem("max_ready")
            self.p_ready = sem("p_ready")
            self.pt_ready = sem("pt_ready")
            self.pt_hi = sem("pt_hi")
            self.pt_copied = sem("pt_copied")
            self.av_done = sem("av_done")
            self.rinv_ready = sem("rinv_ready")
            self.o_ready = sem("o_ready")
            self.oT_hi = sem("oT_hi")
            self.oT_done = sem("oT_done")
            self.v_hi = sem("v_hi")
            self.v_ready = sem("v_ready")
            self.vbias = DH == 16 and not cross
            if self.vbias:
                self.v_raw = sem("v_raw")
            self.qk_raw = sem("qk_raw")
            self.qk_out = sem("qk_out")
            if rope:
                self.rope_step = sem("rope_step")
            if cross:
                self.ctx_in = [sem(f"ctx_in{k}") for k in (0, 1)]
                self.chat_ready = sem("chat_ready")
                self.c_f32 = sem("c_f32")
                self.c_hi = sem("c_hi")
                self.cT_ready = sem("cT_ready")
                if rope:
                    self.ctx_stats = sem("ctx_stats")
                    self.ctx_sums = sem("ctx_sums")
                    self.ctx_veps = sem("ctx_veps")
                    self.ctx_rstd = sem("ctx_rstd")
                else:
                    self.c_raw = sem("c_raw")
        else:
            self.g_f32 = sem("g_f32")
            self.g_hi = sem("g_hi")
            self.g_ready = sem("g_ready")

    def stats(self, whose):
        return [(whose, w, 0) for w in ["LN"] + ["CN"] * self.cross]

    def norms(self, whose):
        return [(whose, w, 0) for w in ["LX"] + ["CX"] * self.cross]

    def turned(self, whose):
        return [(whose, w, 0) for w in ["LNT"] + ["CT"] * self.cross]

    def queries_keys(self):
        qk = [("next", "QK", j) for j in range(self.NQK)] if self.att else []
        if self.cross and not self.rope:
            qk.insert(1, ("next", "CP", 0))
        return qk

    def values(self):
        return [("next", "V", j) for j in range(self.NV)] if self.att else []

    def at_time(self, n):
        return [(what, n - lag) for what, lag in (("S", 0), ("T", 2), ("E", 0), ("AV", 4)) if 0 <= n - lag < self.U]

    def head(self):
        return [("next",) + s for n in range(self.ahead) for s in self.at_time(n)] if self.att else []

    def first_steps(self):
        split = [("next", "W", (self, c)) for c in range(EARLY_CHUNKS, self.chunks)]
        out = self.stats("next") + self.norms("next") + [("next", "XB", 0), ("next", "MOD", 0)]
        for step in self.turned("next") + self.queries_keys():
            out += split[:1] + [step]
            split = split[1:]
        return out + self.values() + self.stats("later") + self.head()

    def steps(self, nxt, later, heavy=None):
        split = [("own", "W", (heavy, c)) for c in range(heavy.chunks)] if heavy else []
        norms = nxt.norms("next") if nxt and not (nxt is self and self.cross) else []
        side = (nxt.turned("next") if norms else []) + nxt.queries_keys() if nxt else []
        early = later is not None and later is nxt and later.cross
        bias = [("next", "XB", 0)] if nxt else []
        values = nxt.values() if nxt else []
        stats = later.stats("later") if later else []
        out = []
        if not self.att:
            out = [("own", "F1", 0)] + norms + bias + [("own", "F1", j) for j in range(1, 4)] + side
            if nxt and nxt.att:
                return out + [("own", "WO", 0)] + values + nxt.head() + stats + split
            return out + [("own", "WO", 0)] + stats + split
        follows = nxt.ahead if nxt and nxt.att else 0
        first_side = self.ahead + (1 if norms else 0)
        last_side = self.U + ((2 if self.cross else 1) if nxt and nxt.att and nxt.rope else -1)
        slots = max(1, min(len(side), last_side - first_side))
        first_value = first_side + slots
        value_slots = max(self.U + (4 if self.cross else 3), first_value + 1) - first_value
        assert first_value + value_slots <= self.U + 4
        end = self.U + max(4, follows)
        due = []
        for n in range(end):
            both = [("own",) + s for s in self.at_time(n)]
            if 0 <= n - self.U < follows:
                both += [("next",) + s for s in nxt.at_time(n - self.U)]
            main = [s for what in ("S", "T", "E") for s in both if s[1] == what]
            products = [s for s in both if s[1] == "AV"]
            if n >= self.ahead:
                out += main
                if n == self.ahead:
                    out += norms + bias
                if n == self.U:
                    out += stats
                if n == end - 2 and early:
                    out += later.norms("later")
                if split:
                    out.append(split.pop(0))
                if first_side <= n < first_side + slots:
                    k = n - first_side
                    out += side[k * len(side) // slots:(k + 1) * len(side) // slots]
                if first_value <= n < first_value + value_slots:
                    k = n - first_value
                    out += values[k * len(values) // value_slots:(k + 1) * len(values) // value_slots]
                while due and due[0][0] <= n:
                    out.append(("own", "OT", due.pop(0)[1]))
                out += products
                if n == end - 1 and early:
                    out += later.turned("later")
            if 4 <= n < self.U + 4 and (n - 4) % self.UI == self.UI - 1:
                due.append((n + 2, (n - 4) // self.UI))
        out += [("own", "OT", n) for _, n in due]
        return out + [("own", "WO", 0)] + split


JOBS = ("LNT", "CT", "CP", "QK", "V", "OT", "F1", "WO")


def count_jobs(steps):
    return sum(s[1] in JOBS for s in steps)


def build(nc, x_dram, ctx_dram, condT, cols, ropes, rows, weights, out):
    with ExitStack() as ctx:
        def sb(name, shape, dtype=F32):
            return ctx.enter_context(nc.sbuf_tensor(name, shape, dtype))

        def sem(name):
            return ctx.enter_context(nc.semaphore(name))

        stages = [
            Stage(nc, ctx, 0, "sa0", "att", 0, 1e-5, DH=64, rope=True, order=0),
            Stage(nc, ctx, 1, "ca0", "att", 0, 1e-5, DH=64, cross=True, rope=True, order=1),
            Stage(nc, ctx, 2, "ff0", "ffn", 1, 1e-5, gelu=ACT.Gelu),
            Stage(nc, ctx, 3, "sa1", "att", 2, 1e-6, DH=16, order=2),
            Stage(nc, ctx, 4, "ca1", "att", 3, 1e-6, DH=16, cross=True, order=3),
            Stage(nc, ctx, 5, "ff1", "ffn", 4, 1e-6, gelu=ACT.Gelu_apprx_tanh),
        ]

        xs = [x_dram] + [nc.dram_tensor(f"x_after_{st.name}", [NB, N, D], F32, kind="Internal").ap()
                       for st in stages[:-1]] + [out]
        coef_dram = nc.dram_tensor("coefs", [5, NB, P, 4], F32, kind="Internal").ap()

        WSIZE = 8192
        wsplit = [sb(f"wsplit{k}", [P, 2, WSIZE], F16) for k in (0, 1)]
        wload = [sb(f"wload{k}", [P, CHUNK]) for k in (0, 1)]
        chunks = []
        for st in stages:
            pieces = {}
            for src, k, n, at in weights[st.index].values():
                for kt in range(k):
                    col_, rows_ = at + kt * n, min(P, src.shape[0] - kt * P)
                    pieces.setdefault(col_ // CHUNK, []).append(
                        (col_ % CHUNK, rows_, n, src[kt * P:kt * P + rows_, :]))
            chunks.append([pieces[c] for c in sorted(pieces)])
            st.chunks = len(pieces)
        colsb = sb("colsb", [P, NCOLS])
        condsb = sb("condsb", [P, KD, NB])
        silub = sb("silub", [P, KD, NB])
        esb = sb("esb", [P, KD, NB])
        modsb = sb("modsb", [P, 20, NB])
        coefsb = sb("coefsb", [P, 5, NB, 4])
        ropesb = sb("ropesb", [P, 4, N])
        rowsb = sb("rowsb", [P, 7, D])
        ident = sb("ident", [P, P])
        headmask = sb("headmask", [P, 8])
        halfpow = sb("halfpow", [P, 2])
        epsb = sb("epsb", [P, 2, TT])
        tick = sb("tick", [P, 1])
        zero = sb("zero", [P, 1])
        bq4 = sb("bq4", [P, 2])

        xt = [sb(f"xt{k}", [P, TT, D]) for k in (0, 1)]
        xb = [sb(f"xb{k}", [P, TT, D]) for k in (0, 1)]
        yt = [sb(f"yt{k}", [P, TT, D]) for k in (0, 1)]
        coef = [sb(f"coef{k}", [P, 4]) for k in (0, 1)]
        ctxt = [sb(f"ctxt{k}", [P, DC]) for k in (0, 1)]
        chat = sb("chat", [P, DC])
        c32 = sb("c32", [P, 2, NC])
        cT = sb("cT", [P, 2, 2, NC], F16)
        cRaw = sb("cRaw", [P, 2, 2, NC], F16)
        stats = sb("stats", [P, TT, 6])
        mv = sb("mv", [P, TT, 2])
        veps = sb("veps", [P, TT])
        rstd = sb("rstd", [P, TT])
        cstats = sb("cstats", [P, 6])
        cmv = sb("cmv", [P, 2])
        cveps = sb("cveps", [P, 1])
        crstd = sb("crstd", [P, 1])
        xhat = sb("xhat", [P, TT, D])
        h32 = sb("h32", [P, KD, N])
        hT = sb("hT", [P, 2, KD, N], F16)
        qT = [sb(f"qT{k}", [P, 8, N]) for k in (0, 1)]
        kbd = [sb(f"kbd{k}", [P, H, N]) for k in (0, 1)]
        ksb = sb("ksb", [P, 2, N])
        v32 = sb("v32", [P, TT, D])
        vaug = [sb(f"vaug{k}", [P, 2, 2 * H * 65], F16) for k in (0, 1)]
        sh = [sb(f"sh{k}", [P, 2 * N]) for k in (0, 1)]
        t1 = [sb(f"t1_{k}", [P, 2 * N]) for k in (0, 1)]
        negmax = [sb(f"negmax{k}", [P, 4]) for k in (0, 1)]
        prob = [sb(f"prob{k}", [P, 512]) for k in (0, 1)]
        probT = [sb(f"probT{k}", [P, 2, 512], F16) for k in range(4)]
        rinv = [sb(f"rinv{k}", [P, H]) for k in (0, 1)]
        osb = [sb(f"osb{k}", [P, 256]) for k in (0, 1)]
        oT = sb("oT", [P, 2, 8, N], F16)

        def bank(name):
            return ctx.enter_context(nc.psum_tensor(name, [P, 512], F32))

        ps_s = [bank("ps_s0"), bank("ps_s1")]
        ps_t = [bank("ps_t0"), bank("ps_t1")]
        ps_o = [bank("ps_o0"), bank("ps_o1")]
        ps_j = [bank("ps_j0"), bank("ps_j1")]

        param_in = sem("param_in")
        ident_step = sem("ident_step")
        silu_step = sem("silu_step")
        mod_mm = sem("mod_mm")
        mod_step = sem("mod_step")
        coef_out = sem("coef_out")
        coef_ready = sem("coef_ready")
        mod_w_in = [sem(f"mod_w_in{k}") for k in (0, 1)]
        kv_blank = sem("kv_blank")
        x_in = [sem(f"x_in{k}") for k in (0, 1)]
        stored = [sem(f"stored{k}") for k in (0, 1)]
        ln_stats = sem("ln_stats")
        ln_sums = sem("ln_sums")
        ln_veps = sem("ln_veps")
        ln_rstd = sem("ln_rstd")
        xhat_ready = sem("xhat_ready")
        xb_ready = sem("xb_ready")
        h_f32 = sem("h_f32")
        h_hi = sem("h_hi")
        h_ready = sem("h_ready")
        w_in = [sem(f"w_in{k}") for k in (0, 1)]
        w_hi = sem("w_hi")
        w_ready = sem("w_ready")
        blank0 = sem("blank0")
        y_ready = sem("y_ready")
        pj_ready = sem("pj_ready")
        pj_free = [sem(f"pj_free{k}") for k in (0, 1)]
        mod_w = {name: kbd[name == "W_ada"][:, :, :].rearrange("p h n -> p (h n)") for name, *_ in weights["mod"]}

        def wview(st, name):
            k, n, at = weights[st.index][name][1:4]
            return wsplit[st.index % 2][:, :, at:at + k * n].rearrange("p s (k n) -> p s k n", k=k)

        def vview(t):
            st = t.st
            return vaug[t.par][:, :, 0:st.KT * H * (st.DH + 1)].rearrange("p s (t h d) -> p s t h d", t=st.KT, h=H)

        def kview(t):
            flat = kbd[t.par][:, :, :].rearrange("p h n -> p (h n)")
            return flat[:, 0:H * t.st.NK].rearrange("p (h n) -> p h n", h=H)

        class Batch:

            def __init__(self, st, i, par):
                self.st, self.i, self.par = st, i, par
                self.B = 2 * i + par
                self.G = 2 * i + (par + NB * st.index)
                self.GP = i + TURNS * st.index

        class Jobs:

            def __init__(self, i, per_turn, at):
                self.i, self.per_turn, self.at = i, per_turn, at

            def slot(self):
                j, self.at = self.at, self.at + 1
                return j % 2, self.i * (self.per_turn // 2) + j // 2, self.i * self.per_turn + j + 1

        def chunks_before(st, c):
            return sum(len(x) for x in chunks[:st.index]) + c

        def loads_before(st, c):
            g = chunks_before(st, c)
            flat = [x for stage_chunks in chunks for x in stage_chunks]
            return sum(len(x) for x in flat[g % 2:g:2])

        def walk(eng, run, enter, begin=None):
            enter(stages[0])
            jobs = Jobs(0, 0, 0)
            run(None, Batch(stages[0], 0, 0), Batch(stages[0], 0, 1), jobs, stages[0].first_steps())
            at = jobs.at
            for s, st in enumerate(stages):
                per = count_jobs(st.steps(st, st))
                if begin:
                    begin(st)
                with eng.Fori(0, TURNS - 1) as i:
                    run(Batch(st, i, 0), Batch(st, i, 1), Batch(st, i + 1, 0), Jobs(i, 2 * per, at),
                        st.steps(st, st))
                    run(Batch(st, i, 1), Batch(st, i + 1, 0), Batch(st, i + 1, 1), Jobs(i, 2 * per, at + per),
                        st.steps(st, st))
                at += (NB - 2) * per
                i = TURNS - 1
                nxt = stages[s + 1] if s + 1 < len(stages) else None
                first, second = (Batch(nxt, 0, 0), Batch(nxt, 0, 1)) if nxt else (None, None)
                run(Batch(st, i, 0), Batch(st, i, 1), first, Jobs(0, 0, at), st.steps(st, nxt, nxt))
                at += count_jobs(st.steps(st, nxt, nxt))
                if nxt:
                    enter(nxt)
                run(Batch(st, i, 1), first, second, Jobs(0, 0, at), st.steps(nxt, nxt))
                at += count_jobs(st.steps(nxt, nxt))

        block = ctx.enter_context(nc.Block())

        @block.sync
        def _(sp):
            sp.dma_start(colsb[:, :], cols).then_inc(param_in, 16)
            sp.dma_start(condsb[:, :, :], condT).then_inc(param_in, 16)
            sp.dma_start(ropesb[:, :, :], ropes).then_inc(param_in, 16)
            sp.dma_start(rowsb[:, :, :], rows.partition_broadcast(P)).then_inc(param_in, 16)
            for name, k, n, at, src in weights["mod"]:
                sp.dma_start(mod_w[name][:, at:at + k * n].rearrange("p (k n) -> p k n", k=k),
                             src.rearrange("(k p) n -> p k n", p=P)).then_inc(mod_w_in[name == "W_ada"], 16)

            def load_x(t, b):
                st = t.st
                if not (st.index == 0 and b is t.par):
                    sp.wait_ge(xhat_ready, t.G - 1)
                    sp.wait_ge(xb_ready, t.G - 1)
                    sp.wait_ge(h_ready, t.G - 1)
                if st.index:
                    sp.wait_ge(stored[t.par], 16 * (t.GP - TURNS + 1) + 1)
                sp.dma_start(xt[t.par][:, :, :], xs[st.index][b].rearrange("(t p) d -> p t d", p=P))\
                    .then_inc(x_in[t.par], 16)
                sp.dma_start(coef[t.par][:, :], coef_dram[st.coef, b]).then_inc(x_in[t.par], 16)
                if st.cross:
                    if b is not t.par:
                        sp.wait_ge(st.chat_ready, t.B - 1)
                    sp.dma_start(ctxt[t.par][0:NC, :], ctx_dram[b]).then_inc(st.ctx_in[t.par], 16)

            def store_y(t, b):
                sp.wait_ge(y_ready, t.G + 1)
                sp.dma_start(xs[t.st.index + 1][b].rearrange("(t p) d -> p t d", p=P), yt[t.par][:, :, :])\
                    .then_inc(stored[t.par], 16)

            for par in (0, 1):
                sp.sem_inc(stored[par], 1)
            sp.wait_ge(coef_ready, 1)
            sp.dma_start(coef_dram[0:2].rearrange("s b p c -> p s b c"), coefsb[:, 0:2, :, :]).then_inc(coef_out, 16)
            sp.wait_ge(coef_out, 16)
            for par in (0, 1):
                load_x(Batch(stages[0], 0, par), par)
            sp.wait_ge(coef_ready, 2)
            sp.dma_start(coef_dram[2:5].rearrange("s b p c -> p s b c"), coefsb[:, 2:5, :, :]).then_inc(coef_out, 16)
            sp.wait_ge(coef_out, 32)
            for s, st in enumerate(stages):
                nxt = stages[s + 1] if s + 1 < len(stages) else None
                with sp.Fori(0, TURNS - 1) as i:
                    for par in (0, 1):
                        load_x(Batch(st, i + 1, par), 2 * i + (2 + par))
                        store_y(Batch(st, i, par), 2 * i + par)
                for par in (0, 1):
                    if nxt:
                        load_x(Batch(nxt, 0, par), par)
                    store_y(Batch(st, TURNS - 1, par), NB - 2 + par)
            for par in (0, 1):
                sp.wait_ge(stored[par], 16 * TURNS * len(stages) + 1)

        @block.gpsimd
        def _(pool):
            g = nc.gpsimd
            g.memset(wload[0][:, :], 0.0)
            g.memset(wload[1][:, :], 0.0).then_inc(blank0, 1)
            g.memset(ident[:, :], 0.0).then_inc(ident_step, 1)
            g.memset(headmask[:, :], 1.0).then_inc(ident_step, 1)
            g.memset(zero[:, :], 0.0)
            g.memset(epsb[:, 0, :], stages[0].eps)
            g.memset(epsb[:, 1, :], stages[3].eps)
            g.memset(halfpow[:, :], -0.5).then_inc(ident_step, 1)
            pool.wait_ge(ident_step, 3)
            g.affine_select(out=ident[:, :], in_=ident[:, :], compare_op=ALU.not_equal, fill=1.0, base=0,
                            pattern=[[-1, P]], channel_multiplier=1).then_inc(ident_step, 1)
            g.affine_select(out=headmask[:, :], in_=headmask[:, :], compare_op=ALU.is_ge, fill=0.0, base=0,
                            pattern=[[-16, 8]], channel_multiplier=1).then_inc(ident_step, 1)
            pool.wait_ge(ident_step, 5)
            g.affine_select(out=headmask[:, :], in_=headmask[:, :], compare_op=ALU.is_ge, fill=0.0, base=15,
                            pattern=[[16, 8]], channel_multiplier=-1).then_inc(ident_step, 1)
            pool.wait_ge(ident_step, 6)

            def blank(st, par):
                t = Batch(st, 0, par)
                g.memset(kbd[par][:, :, :], 0.0)
                for kt in range(st.KT):
                    g.memset(vview(t)[:, HI, kt, :, st.DH], 1.0)
                    last = g.memset(vview(t)[:, LO, kt, :, st.DH], 0.0)
                last.then_inc(kv_blank, 1)
                pool.wait_ge(kv_blank, 2 * st.order + par + 1)

            def enter(st):
                if st.att:
                    if st.index:
                        pool.wait_ge(y_ready, NB * st.index - 1)
                    else:
                        pool.wait_ge(mod_mm, 1)
                    blank(st, 0)

            def norm_rstd(t):
                pool.wait_ge(ln_sums, t.G + 1)
                g.tensor_tensor(veps[:, :], mv[:, :, 1], epsb[:, t.st.index // 3, :], ALU.add)\
                    .then_inc(ln_veps, 1)
                pool.wait_ge(ln_veps, t.G + 1)
                g.tensor_tensor(rstd[:, :], veps[:, :], halfpow[:, :], ALU.pow).then_inc(ln_rstd, 1)

            def add_bias(t):
                pool.wait_ge(x_in[t.par], 32 * (t.GP + 1))
                if t.st.cross:
                    pool.wait_ge(y_ready, t.G - 1)
                else:
                    pool.wait_ge(xhat_ready, t.G + 1)
                g.tensor_tensor(xb[t.par][:, :, :], xt[t.par][:, :, :],
                                rowsb[:, t.st.index, :].unsqueeze(1).to_broadcast([P, TT, D]), ALU.add)\
                    .then_inc(xb_ready, 1)

            def ctx_norm_rstd(t):
                st = t.st
                pool.wait_ge(st.ctx_sums, t.B + 1)
                g.tensor_tensor(cveps[0:NC, :], cmv[0:NC, 1:2], epsb[0:NC, 0, 0:1], ALU.add)\
                    .then_inc(st.ctx_veps, 1)
                pool.wait_ge(st.ctx_veps, t.B + 1)
                g.tensor_tensor(crstd[0:NC, :], cveps[0:NC, :], halfpow[0:NC, 0:1], ALU.pow)\
                    .then_inc(st.ctx_rstd, 1)

            def finish_qk(t, j):
                st, B = t.st, t.B
                kv = kview(t)
                if st.rope:
                    isk = j % 2
                    cols_ = st.NK if isk else N
                    m = 2 * (j // 2)
                    view = lambda buf: buf[:, 0:2 * cols_].rearrange("p (m n) -> p m n", m=2)
                    pool.wait_ge(st.qk_raw, B * st.NQK + j + 1)
                    sin = ropesb[:, 3 if isk else 1, 0:cols_].unsqueeze(1).to_broadcast([P, 2, cols_])
                    g.tensor_tensor(view(sh[j % 2]), view(sh[j % 2]), sin, ALU.mult).then_inc(st.rope_step, 1)
                    pool.wait_ge(st.rope_step, B * st.NQK + j + 1)
                    if not isk:
                        g.tensor_tensor(qT[t.par][:, m:m + 2, :], view(t1[j % 2]), view(sh[j % 2]), ALU.add)\
                            .then_inc(st.qk_out, 1)
                    else:
                        for hh in (0, 1):
                            r = slice(64 * hh, 64 * hh + 64)
                            dst = kv[r, 2 * m + hh:2 * m + 4:2, :]
                            last = g.tensor_tensor(dst, view(t1[j % 2])[r], view(sh[j % 2])[r], ALU.add)
                        last.then_inc(st.qk_out, 1)
                        pool.wait_ge(st.qk_out, B * st.NQK + j + 1)
                elif j == 1:
                    pool.wait_ge(st.qk_raw, B * 2 + 2)
                    for m in (0, 1):
                        last = g.tensor_tensor(
                            kv[:, 8 * m:8 * m + 8, :],
                            ksb[:, m, 0:st.NK].unsqueeze(1).to_broadcast([P, 8, st.NK]),
                            headmask[:, :].unsqueeze(2).to_broadcast([P, 8, st.NK]), ALU.mult)
                        last.then_inc(st.qk_out, 1)

            def run(own, nxt, later, jobs, steps):
                for whose, what, j in steps:
                    t = {"own": own, "next": nxt, "later": later}[whose]
                    if what == "LN":
                        norm_rstd(t)
                    elif what == "CN" and t.st.rope:
                        ctx_norm_rstd(t)
                    elif what == "XB":
                        add_bias(t)
                    elif what == "QK":
                        finish_qk(nxt, j)

            def begin(st):
                if st.att:
                    if st.index:
                        pool.wait_ge(y_ready, NB * st.index)
                    else:
                        pool.wait_ge(mod_mm, 2)
                    blank(st, 1)

            walk(pool, run, enter, begin)

        @block.scalar
        def _(act):
            a = nc.scalar
            def load_chunk(st, c):
                for col_, rows_, n, src in chunks[st.index][c]:
                    act.dma_start(wload[chunks_before(st, c) % 2][0:rows_, col_:col_ + n], src)\
                        .then_inc(w_in[chunks_before(st, c) % 2], 16)

            def split_chunk(ws, c):
                at = chunks_before(ws, c)
                if 1 <= c < ws.chunks - 1:
                    act.wait_ge(w_ready, at)
                    load_chunk(ws, c + 1)
                act.wait_ge(w_in[at % 2], 16 * (loads_before(ws, c) + len(chunks[ws.index][c])))
                a.activation(wsplit[ws.index % 2][:, HI, c * CHUNK:(c + 1) * CHUNK],
                             wload[at % 2][:, :], ACT.Copy, scale=W_SCALE).then_inc(w_hi, 1)

            def begin(st):
                if st.index + 1 < len(stages):
                    nxt = stages[st.index + 1]
                    act.wait_ge(w_ready, chunks_before(nxt, 0))
                    for c in range(2):
                        load_chunk(nxt, c)

            act.wait_ge(blank0, 1)
            for c in range(2):
                load_chunk(stages[0], c)
            act.wait_ge(param_in, 64)
            a.activation(esb[:, :, :], condsb[:, :, :], ACT.Exp, scale=-1.0).then_inc(silu_step, 1)
            a.activation(bq4[:, :], colsb[:, COLS["b_qk"]:COLS["b_qk"] + 2], ACT.Copy, scale=0.25)\
                .then_inc(silu_step, 1)
            act.wait_ge(silu_step, 2)
            for c in range(EARLY_CHUNKS):
                split_chunk(stages[0], c)

            def col(name, c, rows_=P):
                return colsb[0:rows_, COLS[name] + c:COLS[name] + c + 1]

            def run(own, nxt, later, jobs, steps):
                    for whose, what, j in steps:
                        t = {"own": own, "next": nxt, "later": later}[whose]
                        st, B = t.st, t.B
                        follows = whose == "next" and own is not None and own.st.att
                        if what in JOBS:
                            k, before, count = jobs.slot()
                            ps = ps_j[k]
                            pv = ps[:, :].rearrange("p (m n) -> p m n", m=2)
                        if what == "W":
                            split_chunk(*j)
                        elif what == "LNT":
                            act.wait_ge(pj_ready, count)
                            act.wait_ge(x_in[t.par], 32 * (t.GP + 1))
                            c = coef[t.par]
                            a.activation(h32[:, 0, :], pv[:, 0, :], ACT.Identity, scale=c[:, 0:1], bias=c[:, 2:3])
                            a.activation(h32[:, 1, :], pv[:, 1, :], ACT.Identity, scale=c[:, 1:2], bias=c[:, 3:4])\
                                .then_inc(h_f32, 1)
                            act.wait_ge(h_f32, t.G + 1)
                            act.sem_inc(pj_free[k], 1)
                            a.activation(hT[:, HI], h32[:, :, :], ACT.Copy).then_inc(h_hi, 1)
                        elif what in ("CT", "CP"):
                            act.wait_ge(pj_ready, count)
                            per = 1 if st.rope else 2
                            nth = B * per + (what == "CP") + 1
                            rows_ = P if what == "CP" else DC - P
                            for m, r in ((0, P), (1, rows_)):
                                src = ps[0:r, m * NC:(m + 1) * NC]
                                if what == "CP":
                                    last = a.activation(c32[0:r, m, :], src, ACT.Identity, scale=1 / W_SCALE,
                                                        bias=col("b_ctx", m))
                                elif st.rope:
                                    last = a.activation(c32[0:r, m, :], src, ACT.Identity,
                                                        scale=col("lnc_w", m, r), bias=col("lnc_b", m, r))
                                else:
                                    last = a.activation(c32[0:r, m, :], src, ACT.Copy)
                            last.then_inc(st.c_f32, 1)
                            act.wait_ge(st.c_f32, nth)
                            act.sem_inc(pj_free[k], 1)
                            dst = cT if what == "CP" or st.rope else cRaw
                            a.activation(dst[:, HI, 0, :], c32[:, 0, :], ACT.Copy)
                            a.activation(dst[0:rows_, HI, 1, :], c32[0:rows_, 1, :], ACT.Copy).then_inc(st.c_hi, 1)
                        elif what == "QK" and not st.rope:
                            act.wait_ge(pj_ready, count)
                            for m in (0, 1):
                                if j == 0:
                                    last = a.activation(qT[t.par][:, m, :], pv[:, m, :], ACT.Identity, scale=0.25 / W_SCALE,
                                                        bias=0.0 if st.cross else bq4[:, m:m + 1])
                                else:
                                    if m == 0 and not (isinstance(B, int) and B == 0):
                                        act.wait_ge(st.qk_out, 2 * B)
                                    last = a.activation(ksb[:, m, 0:st.NK], ps[:, m * st.NK:(m + 1) * st.NK],
                                                        ACT.Identity, scale=1 / W_SCALE,
                                                        bias=0.0 if st.cross else col("b_qk", 2 + m))
                            last.then_inc(st.qk_raw, 1)
                            act.wait_ge(st.qk_raw, B * 2 + j + 1)
                            act.sem_inc(pj_free[k], 1)
                        elif what == "V":
                            if st.vbias:
                                act.wait_ge(st.v_raw, B + 1)
                                for tt in range(TT):
                                    last = a.activation(vview(t)[:, HI, tt, :, 0:16],
                                                        v32[:, tt, :].rearrange("p (h d) -> p h d", h=H), ACT.Copy)
                            else:
                                act.wait_ge(pj_ready, count)
                                tt, h0, nh = (j % st.KT, 8 * (j // st.KT), 8) if st.DH == 64 else (0, 0, H)
                                last = a.activation(vview(t)[0:st.KP, HI, tt, h0:h0 + nh, 0:st.DH],
                                                    ps[0:st.KP, 0:nh * st.DH].rearrange("p (h d) -> p h d", h=nh),
                                                    ACT.Copy, scale=1 / W_SCALE)
                            last.then_inc(st.v_hi, 1)
                        elif what == "E":
                            act.wait_ge(st.max_ready, B * st.U + j + 1)
                            if j >= 2:
                                act.wait_ge(st.pt_ready, B * st.U + j - 1)
                            elif follows:
                                act.wait_ge(own.st.pt_ready, (own.B + 1) * own.st.U + j - 1)
                            for hh in range(st.HU):
                                c = slice(hh * st.NK, (hh + 1) * st.NK)
                                last = a.activation(prob[j % 2][:, c], ps_s[j % 2][:, c], ACT.Exp,
                                                    bias=negmax[j % 2][:, hh:hh + 1])
                            last.then_inc(st.p_ready, 1)
                        elif what == "T":
                            act.wait_ge(st.pt_ready, B * st.U + j + 1)
                            if j >= 4:
                                act.wait_ge(st.av_done, B * st.U + j - 3)
                            elif follows:
                                act.wait_ge(own.st.av_done, (own.B + 1) * own.st.U + j - 3)
                            a.activation(probT[j % 4][0:st.KP, HI, :], ps_t[j % 2][0:st.KP, :], ACT.Copy,
                                         scale=P_SCALE).then_inc(st.pt_hi, 1)
                        elif what == "OT":
                            act.wait_ge(pj_ready, count)
                            g_, tt = j // TT, j % TT
                            a.activation(oT[:, HI, 2 * g_:2 * g_ + 2, tt * P:tt * P + P],
                                         ps[:, 0:256].rearrange("p (f n) -> p f n", f=2), ACT.Copy)\
                                .then_inc(st.oT_hi, 1)
                        elif what == "F1":
                            act.wait_ge(pj_ready, count)
                            if j >= 2:
                                act.wait_ge(st.g_ready, B * 4 + j - 1)
                            name = "ff_b1" if st.index == 2 else "b_fc1"
                            for m in (0, 1):
                                last = a.activation(t1[j % 2][:, m * N:(m + 1) * N], pv[:, m, :], st.gelu,
                                                    scale=1 / W_SCALE, bias=col(name, 2 * j + m))
                            last.then_inc(st.g_f32, 1)
                            act.wait_ge(st.g_f32, B * 4 + j + 1)
                            act.sem_inc(pj_free[k], 1)
                            a.activation(oT[:, HI, 2 * j:2 * j + 2, :],
                                         t1[j % 2][:, :].rearrange("p (m n) -> p m n", m=2), ACT.Copy)\
                                .then_inc(st.g_hi, 1)

            walk(act, run, lambda st: None, begin)

        @block.vector
        def _(dve):
            v = nc.vector
            dve.wait_ge(silu_step, 2)
            v.tensor_scalar(esb[:, :, :], esb[:, :, :], 1.0, None, ALU.add).then_inc(mod_step, 1)
            dve.wait_ge(mod_step, 1)
            v.reciprocal(esb[:, :, :], esb[:, :, :]).then_inc(mod_step, 1)
            dve.wait_ge(mod_step, 2)
            v.tensor_tensor(silub[:, :, :], esb[:, :, :], condsb[:, :, :], ALU.mult).then_inc(mod_step, 1)

            def split_chunk(ws, c):
                at = chunks_before(ws, c)
                dve.wait_ge(w_hi, at + 1)
                dst = wsplit[ws.index % 2][:, :, c * CHUNK:(c + 1) * CHUNK]
                v.scalar_tensor_tensor(dst[:, LO], wload[at % 2][:, :], W_SCALE, dst[:, HI],
                                       ALU.mult, ALU.subtract).then_inc(w_ready, 1)

            def modulation(vectors, coefs, bank):
                bias_at = [COLS["g1_b"] + c for c in range(8)] + [COLS["b_ada"] + c for c in range(12)]
                gains = (0, 1, 4, 5, 10, 11, 14, 15, 18, 19)
                dve.wait_ge(mod_mm, bank + 1)
                for n, c in enumerate(vectors):
                    at = bias_at[c]
                    last = v.tensor_scalar(modsb[:, c, :], ps_j[bank][:, n * NB:(n + 1) * NB], colsb[:, at:at + 1],
                                           1.0 if c in gains else 0.0, ALU.add, ALU.add)
                last.then_inc(mod_step, 1)
                dve.wait_ge(mod_step, 4 + bank)
                dve.sem_inc(pj_free[bank], 1)
                for s in coefs:
                    for k in range(KD):
                        if s < 2:
                            w = colsb[:, COLS[("ln1_w", "ln2_w")[s]] + k:COLS[("ln1_w", "ln2_w")[s]] + k + 1]
                            b_ = colsb[:, COLS[("ln1_b", "ln2_b")[s]] + k:COLS[("ln1_b", "ln2_b")[s]] + k + 1]
                            gain, shift = modsb[:, 4 * s + k, :], modsb[:, 4 * s + 2 + k, :]
                            v.tensor_scalar(coefsb[:, s, :, k], gain, w, None, ALU.mult)
                            last = v.scalar_tensor_tensor(coefsb[:, s, :, 2 + k], gain, b_, shift, ALU.mult, ALU.add)
                        else:
                            c = 8 + 4 * (s - 2)
                            v.tensor_copy(coefsb[:, s, :, k], modsb[:, c + 2 + k, :])
                            last = v.tensor_copy(coefsb[:, s, :, 2 + k], modsb[:, c + k, :])
                last.then_inc(coef_ready, 1)

            for c in range(2):
                split_chunk(stages[0], c)
            modulation(range(0, 8), range(0, 2), 0)
            for c in range(2, EARLY_CHUNKS):
                split_chunk(stages[0], c)
            dve.wait_ge(param_in, 64)
            dve.wait_ge(ident_step, 6)

            def norm(t):
                xs_ = xt[t.par]
                dve.wait_ge(x_in[t.par], 32 * (t.GP + 1))
                for tt in range(TT):
                    last = v.bn_stats(stats[:, tt, :], xs_[:, tt, :])
                last.then_inc(ln_stats, 1)
                dve.wait_ge(ln_stats, t.G + 1)
                v.memset(tick[:, :], 0.0)
                for tt in range(TT):
                    last = v.bn_aggr(mv[:, tt, :], stats[:, tt, :])
                last.then_inc(ln_sums, 1)

            def normalise(t):
                xs_ = xt[t.par]
                dve.wait_ge(ln_rstd, t.G + 1)
                if not (isinstance(t.G, int) and t.G == 0):
                    dve.wait_ge(h_ready, t.G)
                for tt in range(TT):
                    last = v.tensor_scalar(xhat[:, tt, :], xs_[:, tt, :], mv[:, tt, 0:1],
                                           rstd[:, tt:tt + 1], ALU.subtract, ALU.mult)
                last.then_inc(xhat_ready, 1)

            def norm_ctx(t):
                st = t.st
                rows_ = ctxt[t.par][0:NC, :]
                dve.wait_ge(st.ctx_in[t.par], 16 * (t.i + 1))
                if st.rope:
                    v.bn_stats(cstats[0:NC, :], rows_).then_inc(st.ctx_stats, 1)
                    dve.wait_ge(st.ctx_stats, t.B + 1)
                    v.memset(tick[:, :], 0.0)
                    v.bn_aggr(cmv[0:NC, :], cstats[0:NC, :]).then_inc(st.ctx_sums, 1)

            def normalise_ctx(t):
                st = t.st
                rows_ = ctxt[t.par][0:NC, :]
                if st.rope:
                    dve.wait_ge(st.ctx_rstd, t.B + 1)
                    v.tensor_scalar(chat[0:NC, :], rows_, cmv[0:NC, 0:1], crstd[0:NC, 0:1],
                                    ALU.subtract, ALU.mult).then_inc(st.chat_ready, 1)
                else:
                    v.tensor_copy(chat[0:NC, :], rows_).then_inc(st.chat_ready, 1)

            def run(own, nxt, later, jobs, steps):
                    for whose, what, j in steps:
                        t = {"own": own, "next": nxt, "later": later}[whose]
                        st, B = t.st, t.B
                        follows = whose == "next" and own is not None and own.st.att
                        if what in JOBS:
                            k, before, count = jobs.slot()
                            ps = ps_j[k]
                        if what == "W":
                            split_chunk(*j)
                        elif what == "MOD":
                            modulation(range(8, 20), range(2, 5), 1)
                        elif what == "LNT":
                            dve.wait_ge(h_hi, t.G + 1)
                            v.tensor_tensor(hT[:, LO], h32[:, :, :], hT[:, HI], ALU.subtract)\
                                .then_inc(h_ready, 1)
                        elif what in ("CT", "CP"):
                            per = 1 if st.rope else 2
                            dve.wait_ge(st.c_hi, B * per + (what == "CP") + 1)
                            dst, done = (cT, st.cT_ready) if what == "CP" or st.rope else (cRaw, st.c_raw)
                            rows_ = P if what == "CP" else DC - P
                            v.tensor_tensor(dst[:, LO, 0, :], c32[:, 0, :], dst[:, HI, 0, :], ALU.subtract)
                            v.tensor_tensor(dst[0:rows_, LO, 1, :], c32[0:rows_, 1, :], dst[0:rows_, HI, 1, :],
                                            ALU.subtract).then_inc(done, 1)
                        elif what == "OT":
                            dve.wait_ge(st.oT_hi, B * st.NO + j + 1)
                            g_, tt = j // TT, j % TT
                            dst = oT[:, :, 2 * g_:2 * g_ + 2, tt * P:tt * P + P]
                            v.tensor_tensor(dst[:, LO], ps[:, 0:256].rearrange("p (f n) -> p f n", f=2),
                                            dst[:, HI], ALU.subtract).then_inc(st.oT_done, 1)
                            dve.wait_ge(st.oT_done, B * st.NO + j + 1)
                            dve.sem_inc(pj_free[k], 1)
                        elif what == "F1":
                            dve.wait_ge(st.g_hi, B * 4 + j + 1)
                            dst = oT[:, :, 2 * j:2 * j + 2, :]
                            v.tensor_tensor(dst[:, LO], t1[j % 2][:, :].rearrange("p (m n) -> p m n", m=2),
                                            dst[:, HI], ALU.subtract).then_inc(st.g_ready, 1)
                        elif what == "LN":
                            norm(t)
                        elif what == "CN":
                            norm_ctx(t)
                        elif what == "LX":
                            normalise(t)
                        elif what == "CX":
                            normalise_ctx(t)
                        elif what == "QK" and st.rope:
                            isk = j % 2
                            n = st.NK if isk else N
                            dve.wait_ge(pj_ready, count)
                            if j >= 2 or not (isinstance(B, int) and B == 0):
                                dve.wait_ge(st.qk_out, B * st.NQK + j - 1)
                            cos = ropesb[:, 2 if isk else 0, 0:n].unsqueeze(1).to_broadcast([P, 2, n])
                            v.tensor_tensor(t1[j % 2][:, 0:2 * n].rearrange("p (m n) -> p m n", m=2),
                                            ps[:, 0:2 * n].rearrange("p (m n) -> p m n", m=2), cos, ALU.mult)
                            v.stream_shuffle(sh[j % 2][:, 0:2 * n], ps[:, 0:2 * n], [c ^ 1 for c in range(32)])\
                                .then_inc(st.qk_raw, 1)
                            dve.wait_ge(st.qk_raw, B * st.NQK + j + 1)
                            dve.sem_inc(pj_free[k], 1)
                        elif what == "V":
                            if st.vbias:
                                dve.wait_ge(pj_ready, count)
                                for tt in range(TT):
                                    last = v.scalar_tensor_tensor(v32[:, tt, :], ps[:, tt * D:(tt + 1) * D],
                                                                  1 / W_SCALE, rowsb[:, 6, :], ALU.mult, ALU.add)
                                last.then_inc(st.v_raw, 1)
                                dve.wait_ge(st.v_hi, B + 1)
                                for tt in range(TT):
                                    dst = vview(t)[:, :, tt, :, 0:16]
                                    last = v.tensor_tensor(dst[:, LO], v32[:, tt, :].rearrange("p (h d) -> p h d", h=H),
                                                           dst[:, HI], ALU.subtract)
                            else:
                                dve.wait_ge(st.v_hi, B * st.NV + j + 1)
                                tt, h0, nh = (j % st.KT, 8 * (j // st.KT), 8) if st.DH == 64 else (0, 0, H)
                                dst = vview(t)[0:st.KP, :, tt, h0:h0 + nh, 0:st.DH]
                                last = v.scalar_tensor_tensor(
                                    dst[:, LO], ps[0:st.KP, 0:nh * st.DH].rearrange("p (h d) -> p h d", h=nh),
                                    1 / W_SCALE, dst[:, HI], ALU.mult, ALU.subtract)
                            last.then_inc(st.v_ready, 1)
                            dve.wait_ge(st.v_ready, B * st.NV + j + 1)
                            dve.sem_inc(pj_free[k], 1)
                        elif what == "S":
                            dve.wait_ge(st.s_ready, B * st.U + j + 1)
                            if j >= 2:
                                dve.wait_ge(st.p_ready, B * st.U + j - 1)
                            elif follows:
                                dve.wait_ge(own.st.p_ready, (own.B + 1) * own.st.U + j - 1)
                            v.tensor_reduce(negmax[j % 2][:, 0:st.HU],
                                            ps_s[j % 2][:, 0:st.HU * st.NK].rearrange("p (h n) -> p h n", h=st.HU),
                                            AX_X, ALU.max, negate=True).then_inc(st.max_ready, 1)
                        elif what == "T":
                            dve.wait_ge(st.pt_hi, B * st.U + j + 1)
                            dst = probT[j % 4][0:st.KP]
                            v.scalar_tensor_tensor(dst[:, LO], ps_t[j % 2][0:st.KP, :], P_SCALE, dst[:, HI],
                                                   ALU.mult, ALU.subtract).then_inc(st.pt_copied, 1)
                        elif what == "AV" and j % st.UI == st.UI - 1:
                            n = j // st.UI
                            dve.wait_ge(st.av_done, B * st.U + j + 1)
                            w = st.DH + 1
                            o = ps_o[n % 2][:, 0:st.HG * w].rearrange("p (h d) -> p h d", h=st.HG)
                            v.reciprocal(rinv[n % 2][:, 0:st.HG], o[:, :, st.DH]).then_inc(st.rinv_ready, 1)
                            dve.wait_ge(st.rinv_ready, B * st.NO + n + 1)
                            if n >= 2:
                                dve.wait_ge(st.oT_done, B * st.NO + n - 1)
                            v.tensor_tensor(osb[n % 2][:, :].rearrange("p (h d) -> p h d", h=st.HG),
                                            o[:, :, 0:st.DH],
                                            rinv[n % 2][:, 0:st.HG].unsqueeze(2).to_broadcast([P, st.HG, st.DH]),
                                            ALU.mult).then_inc(st.o_ready, 1)
                        elif what == "WO":
                            dve.wait_ge(pj_ready, count)
                            dve.wait_ge(xb_ready, t.G + 1)
                            dve.wait_ge(stored[t.par], 16 * t.GP + 1)
                            v.scalar_tensor_tensor(yt[t.par][:, :, :], ps[:, :].rearrange("p (t d) -> p t d", t=TT),
                                                   1 / W_SCALE, xb[t.par][:, :, :], ALU.mult, ALU.add)\
                                .then_inc(y_ready, 1)
                            dve.wait_ge(y_ready, t.G + 1)
                            dve.sem_inc(pj_free[k], 1)

            walk(dve, run, lambda st: None)

        @block.tensor
        def _(pe):
            te = nc.tensor
            pe.wait_ge(param_in, 64)
            pe.wait_ge(mod_w_in[0], 16 * (len(weights["mod"]) - 1))
            pe.wait_ge(mod_step, 3)
            tile = 0
            for name, k_, n_, at, _src in weights["mod"]:
                if name == "W_ada":
                    last.then_inc(mod_mm, 1)
                    pe.wait_ge(mod_w_in[1], 16)
                w = mod_w[name][:, at:at + k_ * n_].rearrange("p (k n) -> p k n", k=k_)
                src = silub if name == "W_ada" else condsb
                for m in range(n_ // P):
                    for k in range(KD):
                        at_ = (tile - 8 if name == "W_ada" else tile) * NB
                        last = te.matmul(ps_j[name == "W_ada"][:, at_:at_ + NB], w[:, k, m * P:(m + 1) * P],
                                         src[:, k, :], start=(k == 0), stop=(k == KD - 1))
                    tile += 1
            last.then_inc(mod_mm, 1)
            pe.wait_ge(ident_step, 6)

            def enter(st):
                if st.index:
                    pe.wait_ge(w_ready, chunks_before(st, st.chunks))

            def project(ps_out, lhsT, rhs, rows_):
                todo = [(k, r, a_, b_) for k, r in enumerate(rows_) for a_, b_ in PARTS]
                for n, (k, r, a_, b_) in enumerate(todo):
                    last = te.matmul(ps_out, lhsT(a_, k, r), rhs(b_, k, r), start=(n == 0),
                                     stop=(n == len(todo) - 1))
                return last

            def run(own, nxt, later, jobs, steps):
                    for whose, what, j in steps:
                        t = {"own": own, "next": nxt, "later": later}[whose]
                        st, B = t.st, t.B
                        follows = whose == "next" and own is not None and own.st.att
                        if what in JOBS:
                            k_, before, _count = jobs.slot()
                            ps = ps_j[k_]
                            pv = ps[:, :].rearrange("p (m n) -> p m n", m=2)
                            pe.wait_ge(pj_free[k_], before + 1)
                        if own is None and what in ("QK", "V"):
                            pe.wait_ge(w_ready, {"QK": 2 if j == 0 else 4, "V": 6}[what])
                        if what == "WO" and st.index == 0:
                            pe.wait_ge(w_ready, st.chunks)
                        if what == "LNT":
                            pe.wait_ge(xhat_ready, t.G + 1)
                            for f in range(KD):
                                for tt in range(TT):
                                    last = te.transpose(pv[:, f, tt * P:(tt + 1) * P],
                                                        xhat[:, tt, f * P:(f + 1) * P], ident[:, :])
                        elif what == "CT":
                            pe.wait_ge(st.chat_ready, B + 1)
                            te.transpose(ps[:, 0:NC], chat[0:NC, 0:P], ident[0:NC, 0:NC])
                            last = te.transpose(ps[0:64, NC:2 * NC], chat[0:NC, P:DC], ident[0:NC, 0:NC])
                        elif what == "CP":
                            pe.wait_ge(st.c_raw, B + 1)
                            w = wview(st, "wctx")
                            for m in (0, 1):
                                last = project(ps[:, m * NC:(m + 1) * NC],
                                               lambda s, k, r: w[0:r, s, k, m * P:(m + 1) * P],
                                               lambda s, k, r: cRaw[0:r, s, k, :], (P, DC - P))
                        elif what == "QK":
                            isk = j % 2
                            if j == 0:
                                pe.wait_ge(h_ready, t.G + 1)
                            if j == 1 and st.cross:
                                pe.wait_ge(st.cT_ready, B + 1)
                            w = wview(st, "wk" if isk else "wq")
                            n = st.NK if isk else N
                            src = cT if isk and st.cross else hT
                            rows_ = (P, DC - P) if isk and st.cross and st.rope else (P, P)
                            for mm in (0, 1):
                                m = 2 * (j // 2) + mm
                                last = project(ps[:, mm * n:(mm + 1) * n],
                                               lambda s, k, r: w[0:r, s, k, m * P:(m + 1) * P],
                                               lambda s, k, r: src[0:r, s, k, 0:n], rows_)
                        elif what == "V":
                            w = wview(st, "wv")
                            src = cT if st.cross else hT
                            rows_ = (P, DC - P) if st.cross and st.rope else (P, P)
                            if st.DH == 64:
                                tt, hf = j % st.KT, j // st.KT
                                last = project(ps[0:st.KP, :],
                                               lambda s, k, r: src[0:r, s, k, tt * P:tt * P + st.KP],
                                               lambda s, k, r: w[0:r, s, k, hf * 512:(hf + 1) * 512], rows_)
                            else:
                                for tt in range(st.KT):
                                    last = project(ps[0:st.KP, tt * 256:(tt + 1) * 256],
                                                   lambda s, k, r: src[0:r, s, k, tt * P:tt * P + st.KP],
                                                   lambda s, k, r: w[0:r, s, k, :], rows_)
                        elif what == "S":
                            if j % (TT * st.UI) == 0:
                                if st.rope:
                                    pe.wait_ge(st.qk_out, B * st.NQK + 2 * (j // (TT * st.UI)) + 2)
                                else:
                                    pe.wait_ge(st.qk_raw, (B + 1) * 2)
                                    pe.wait_ge(st.qk_out, 2 * B + 1)
                            elif j == st.UI // 2 and not st.rope:
                                pe.wait_ge(st.qk_out, 2 * B + 2)
                            if j >= 2:
                                pe.wait_ge(st.p_ready, B * st.U + j - 1)
                            elif follows:
                                pe.wait_ge(own.st.p_ready, (own.B + 1) * own.st.U + j - 1)
                            grp, rest = j // (TT * st.UI), j % (TT * st.UI)
                            tt, h0 = rest // st.UI, grp * st.HG + (rest % st.UI) * st.HU
                            kv = kview(t)
                            step = min(st.HU, st.TH)
                            for h in range(h0, h0 + st.HU, step):
                                c = (h - h0) * st.NK
                                last = te.matmul(ps_s[j % 2][:, c:c + step * st.NK],
                                                 qT[t.par][:, h // st.TH, tt * P:(tt + 1) * P],
                                                 kv[:, h:h + step, :], start=True, stop=True)
                            last.then_inc(st.s_ready, 1)
                        elif what == "T":
                            pe.wait_ge(st.p_ready, B * st.U + j + 1)
                            if j >= 2:
                                pe.wait_ge(st.pt_copied, B * st.U + j - 1)
                            elif follows:
                                pe.wait_ge(own.st.pt_copied, (own.B + 1) * own.st.U + j - 1)
                            for blk in range(4):
                                last = te.transpose(ps_t[j % 2][0:st.KP, blk * P:(blk + 1) * P],
                                                    prob[j % 2][:, blk * st.KP:(blk + 1) * st.KP], ident[:, :])
                            last.then_inc(st.pt_ready, 1)
                        elif what == "AV":
                            if j % (st.U // 2) == 0:
                                halves = 2 if st.NV == 1 else 1 + 2 * j // st.U
                                pe.wait_ge(st.v_ready, B * st.NV + halves * st.NV // 2)
                            if j == 0:
                                pe.wait_ge(kv_blank, 2 * st.order + t.par + 1)
                            pe.wait_ge(st.pt_copied, B * st.U + j + 1)
                            n = j // st.UI
                            if j % st.UI == 0:
                                if n >= 2:
                                    pe.wait_ge(st.o_ready, B * st.NO + n - 1)
                                elif follows:
                                    pe.wait_ge(own.st.o_ready, (own.B + 1) * own.st.NO + n - 1)
                            grp, rest = j // (TT * st.UI), j % (TT * st.UI)
                            w = st.DH + 1
                            for hh in range(st.HU):
                                pos = (rest % st.UI) * st.HU + hh
                                for kt in range(st.KT):
                                    blk = hh * st.KT + kt
                                    for n_part, (pp, vp) in enumerate(PARTS):
                                        last = te.matmul(ps_o[n % 2][:, pos * w:(pos + 1) * w],
                                                         probT[j % 4][0:st.KP, pp, blk * P:(blk + 1) * P],
                                                         vview(t)[0:st.KP, vp, kt, grp * st.HG + pos, :],
                                                         start=(kt == 0 and n_part == 0),
                                                         stop=(kt == st.KT - 1 and n_part == 2))
                            last.then_inc(st.av_done, 1)
                        elif what == "OT":
                            pe.wait_ge(st.o_ready, B * st.NO + j + 1)
                            for f in (0, 1):
                                last = te.transpose(ps[:, f * P:(f + 1) * P], osb[j % 2][:, f * P:(f + 1) * P],
                                                    ident[:, :])
                        elif what == "F1":
                            if j == 0:
                                pe.wait_ge(h_ready, t.G + 1)
                            w = wview(st, "w1")
                            for mm in (0, 1):
                                m = 2 * j + mm
                                last = project(pv[:, mm, :], lambda s, k, r: w[:, s, k, m * P:(m + 1) * P],
                                               lambda s, k, r: hT[:, s, k, :], (P, P))
                        elif what == "WO":
                            w = wview(st, "wo")
                            kt_n = st.M if st.att else 8
                            for tt in range(TT):
                                if st.att:
                                    pe.wait_ge(st.oT_done, B * st.NO + st.NO - TT + tt + 1)
                                for kt in range(kt_n):
                                    if not st.att and tt == 0 and kt % 2 == 0:
                                        pe.wait_ge(st.g_ready, B * 4 + kt // 2 + 1)
                                    for n_part, (a_, b_) in enumerate(PARTS):
                                        last = te.matmul(pv[:, tt, :], oT[:, a_, kt, tt * P:(tt + 1) * P],
                                                         w[:, b_, kt, :], start=(kt == 0 and n_part == 0),
                                                         stop=(kt == kt_n - 1 and n_part == 2))
                        if what in JOBS:
                            last.then_inc(pj_ready, 1)

            walk(pe, run, enter)


def kernel(**inputs):
    import concourse.bacc as _bacc
    from concourse import mybir as _mybir
    from concourse.bass_utils import run_bass_kernel_spmd as _run

    nc = _bacc.Bacc("TRN2", target_bir_lowering=False, num_devices=1)
    arrays = {}

    def dram(name, a):
        a = np.ascontiguousarray(a)
        arrays[name] = a
        return nc.dram_tensor(name, a.shape, _mybir.dt.from_np(a.dtype), kind="ExternalInput").ap()

    L0, L1 = "L0_xcond_", "L1_xcond_"
    g = {k: np.asarray(v) for k, v in inputs.items()}

    def columns(v):
        v = np.concatenate([v, np.zeros((-len(v)) % P, v.dtype)])
        return v.reshape(-1, P).T

    qkv_b = g[L1 + "b_qkv"]
    order = [g[L0 + "ln1_w"], g[L0 + "ln1_b"], g[L0 + "ln2_w"], g[L0 + "ln2_b"], g[L0 + "g1_b"], g[L0 + "b1_b"],
             g[L0 + "g2_b"], g[L0 + "b2_b"], g[L0 + "ca_lnc_w"], g[L0 + "ca_lnc_b"], g[L0 + "ff_b1"],
             g[L1 + "b_ada"], qkv_b[0:2 * D], g[L1 + "b_ctx"], g[L1 + "b_fc1"]]
    cols = dram("in_cols", np.concatenate([columns(v) for v in order], axis=1))
    condT = dram("in_condT", g["cond_1024"].reshape(NB, KD, P).transpose(2, 1, 0))
    rows = dram("in_rows", np.stack([g[L0 + "sa_bo"], g[L0 + "ca_bo"], g[L0 + "ff_b2"], g[L1 + "b_proj"],
                                     g[L1 + "b_out"], g[L1 + "b_fc2"], qkv_b[2 * D:3 * D]]))

    f32 = np.float32
    inv = (f32(1.0) / np.power(f32(10000.0), np.arange(0, 64, 2, dtype=f32) / f32(64))).astype(f32)
    ang = (np.arange(N, dtype=f32)[:, None] * inv[None, :]).astype(f32)
    sin, cos = np.sin(ang.astype(np.float64)), np.cos(ang.astype(np.float64))
    freq = (np.arange(P) % 64) // 2
    sign = np.where(np.arange(P) % 2 == 0, -1.0, 1.0)[:, None]
    c, s = cos.T[freq], sin.T[freq] * sign
    ropes = dram("in_ropes", (np.stack([c * 0.125, s * 0.125, c, s], axis=1) / W_SCALE).astype(f32))

    def w(name):
        return dram("in_" + name, g[name])

    def place(*items):
        out, at = {}, 0
        for name, src, n in items:
            k = -(-src.shape[0] // P)
            out[name] = (src, k, n, at)
            at += k * n
        return out

    sakv, cakv, qkv = w(L0 + "sa_wkv"), w(L0 + "ca_wkv"), w(L1 + "W_qkv")
    weights = {
        0: place(("wq", w(L0 + "sa_wq"), 1024), ("wk", sakv[:, 0:1024], 1024), ("wv", sakv[:, 1024:2048], 1024),
                 ("wo", w(L0 + "sa_wo"), 256)),
        1: place(("wq", w(L0 + "ca_wq"), 1024), ("wk", cakv[:, 0:1024], 1024), ("wv", cakv[:, 1024:2048], 1024),
                 ("wo", w(L0 + "ca_wo"), 256)),
        2: place(("w1", w(L0 + "ff_w1"), 1024), ("wo", w(L0 + "ff_w2"), 256)),
        3: place(("wq", qkv[:, 0:256], 256), ("wk", qkv[:, 256:512], 256), ("wv", qkv[:, 512:768], 256),
                 ("wo", w(L1 + "W_proj"), 256)),
        4: place(("wctx", w(L1 + "W_ctx"), 256), ("wq", w(L1 + "W_q"), 256), ("wk", w(L1 + "W_k"), 256),
                 ("wv", w(L1 + "W_v"), 256), ("wo", w(L1 + "W_out"), 256)),
        5: place(("w1", w(L1 + "W_fc1"), 1024), ("wo", w(L1 + "W_fc2"), 256)),
    }
    mod, at = [], 0
    for name in ("g1_w", "b1_w", "g2_w", "b2_w", "W_ada"):
        src = w((L1 if name == "W_ada" else L0) + name)
        mod.append((name, KD, src.shape[1], at if name != "W_ada" else 0, src))
        at += KD * src.shape[1]
    weights["mod"] = mod
    x = dram("in_x", g["x"])
    context = dram("in_ctx", g["ctx_768"])
    out = nc.dram_tensor("out_0", [NB, N, D], _mybir.dt.float32, kind="ExternalOutput").ap()
    build(nc, x, context, condT, cols, ropes, rows, weights, out)
    r = _run(nc, [arrays], core_ids=[0])
    return r.results[0]["out_0"]
```
